# Optimizing a Trainium2 kernel written in Bass

```python
import numpy as np
import jax
import jax.numpy as jnp

def _softmax(x, axis=-1):
    return jax.nn.softmax(x, axis=axis)

def _gelu(x):
    return jax.nn.gelu(x, approximate=True)

def _silu(x):
    return jax.nn.silu(x)

def _sigmoid(x):
    return jax.nn.sigmoid(x)

def _layernorm(x, axis=-1, eps=1e-05):
    m = jnp.mean(x, axis=axis, keepdims=True)
    v = jnp.var(x, axis=axis, keepdims=True)
    return (x - m) / jnp.sqrt(v + eps)

def _scatter_add(tgt, idx, src, axis=0):
    return tgt.at[idx].add(src)

def _segment_sum(src, seg, n):
    return jax.ops.segment_sum(src, seg, n)
kernel_name = 'mk_conv_attn_hybrid_d2_conv_nchw256_r4_20bed1'

def setup_inputs(seed: int=0):
    np.random.seed(seed)
    _w = jnp.asarray

    def _rec_inputs():
        import jax
        import jax.numpy as jnp
        _gk = jax.random.key(seed)
        x = 7.22e-05 + 1 * jax.random.normal(jax.random.fold_in(_gk, 1), (8, 64, 16, 16), jnp.float32)
        return x
    x = _rec_inputs()

    def _L0_conv_setup():
        import jax, jax.numpy as jnp
        import numpy as np
        C = 64
        K_SIZE = 3
        GROUPS = 16
        HIDDEN = C // 4
        B, H, W = (8, 16, 16)
        key = jax.random.key(seed)
        k0, k1, k2 = jax.random.split(key, 3)
        kk = K_SIZE * K_SIZE
        return {'x': jax.random.normal(k0, (B, C, H, W), dtype=jnp.float32), 'w_reduce': jax.random.normal(k1, (HIDDEN, C), dtype=jnp.float32) * 0.05, 'b_reduce': jnp.zeros((HIDDEN,), dtype=jnp.float32), 'w_span': jax.random.normal(k2, (GROUPS * kk, HIDDEN), dtype=jnp.float32) * 0.05, 'b_span': jnp.zeros((GROUPS * kk,), dtype=jnp.float32)}
    _L0_conv_all = _L0_conv_setup()
    _L0_conv_in = {k: v for k, v in _L0_conv_all.items() if k in ('w_reduce', 'b_reduce', 'w_span', 'b_span')}
    del _L0_conv_all

    def _L1_attn_setup():
        import jax, jax.numpy as jnp
        import numpy as np
        F_DIM = 64
        key = jax.random.key(seed)
        ks = jax.random.split(key, 8)
        B, S, F = (8, 512, F_DIM)
        scale = 1.0 / np.sqrt(F)
        return {'x': jax.random.normal(ks[0], (B, S, F), dtype=jnp.float32), 'att_w': jax.random.normal(ks[1], (3 * F,), dtype=jnp.float32) * scale, 'z_w': jax.random.normal(ks[2], (F, 2 * F), dtype=jnp.float32) * scale, 'z_b': jax.random.normal(ks[3], (F,), dtype=jnp.float32) * 0.01, 'r_w': jax.random.normal(ks[4], (F, 2 * F), dtype=jnp.float32) * scale, 'r_b': jax.random.normal(ks[5], (F,), dtype=jnp.float32) * 0.01, 'f_w': jax.random.normal(ks[6], (F, 2 * F), dtype=jnp.float32) * scale, 'f_b': jax.random.normal(ks[7], (F,), dtype=jnp.float32) * 0.01}
    _L1_attn_all = _L1_attn_setup()
    _L1_attn_in = {k: v for k, v in _L1_attn_all.items() if k in ('att_w', 'z_w', 'z_b', 'r_w', 'r_b', 'f_w', 'f_b')}
    del _L1_attn_all

    def _L1_ffn_setup():
        import jax, jax.numpy as jnp
        import numpy as np
        N_EXPERTS = 8
        TOP_K = 2
        key = jax.random.key(seed)
        ks = jax.random.split(key, 5)
        B, T, C, E, H = (8, 512, 64, 8, 682)
        scale = 1.0 / np.sqrt(C)
        return {'x': jax.random.normal(ks[0], (B, T, C), dtype=jnp.float32), 'router_w': jax.random.normal(ks[1], (E, C), dtype=jnp.float32) * scale, 'w1': jax.random.normal(ks[2], (E, H, C), dtype=jnp.float32) * scale, 'w2': jax.random.normal(ks[3], (E, C, H), dtype=jnp.float32) * (1.0 / np.sqrt(H)), 'w3': jax.random.normal(ks[4], (E, H, C), dtype=jnp.float32) * scale}
    _L1_ffn_all = _L1_ffn_setup()
    _L1_ffn_in = {k: v for k, v in _L1_ffn_all.items() if k in ('router_w', 'w1', 'w2', 'w3')}
    del _L1_ffn_all
    return {'x': x, 'L0_conv_w_reduce': _L0_conv_in['w_reduce'], 'L0_conv_b_reduce': _L0_conv_in['b_reduce'], 'L0_conv_w_span': _L0_conv_in['w_span'], 'L0_conv_b_span': _L0_conv_in['b_span'], 'L1_attn_att_w': _L1_attn_in['att_w'], 'L1_attn_z_w': _L1_attn_in['z_w'], 'L1_attn_z_b': _L1_attn_in['z_b'], 'L1_attn_r_w': _L1_attn_in['r_w'], 'L1_attn_r_b': _L1_attn_in['r_b'], 'L1_attn_f_w': _L1_attn_in['f_w'], 'L1_attn_f_b': _L1_attn_in['f_b'], 'L1_ffn_router_w': _L1_ffn_in['router_w'], 'L1_ffn_w1': _L1_ffn_in['w1'], 'L1_ffn_w2': _L1_ffn_in['w2'], 'L1_ffn_w3': _L1_ffn_in['w3']}

def reference(x, L0_conv_w_reduce, L0_conv_b_reduce, L0_conv_w_span, L0_conv_b_span, L1_attn_att_w, L1_attn_z_w, L1_attn_z_b, L1_attn_r_w, L1_attn_r_b, L1_attn_f_w, L1_attn_f_b, L1_ffn_router_w, L1_ffn_w1, L1_ffn_w2, L1_ffn_w3):
    import jax
    import jax.numpy as jnp

    def _L0_conv_ref(x, w_reduce, b_reduce, w_span, b_span):
        import jax, jax.numpy as jnp
        import numpy as np
        C = 64
        K_SIZE = 3
        GROUPS = 16
        HIDDEN = C // 4
        B, H, W = (8, 16, 16)
        b, c, h, w = x.shape
        k, g = (K_SIZE, GROUPS)
        kk = k * k
        hid = jax.nn.relu(jnp.einsum('oc,bcxy->boxy', w_reduce, x) + b_reduce[None, :, None, None])
        Kmap = jnp.einsum('oc,bcxy->boxy', w_span, hid) + b_span[None, :, None, None]
        Kmap = Kmap.reshape(b, g, kk, h, w)
        pad = k // 2
        xp = jnp.pad(x, ((0, 0), (0, 0), (pad, pad), (pad, pad)))
        patches = jnp.stack([xp[:, :, i:i + h, j:j + w] for i in range(k) for j in range(k)], axis=2)
        patches = patches.reshape(b, g, c // g, kk, h, w)
        out = jnp.einsum('bgnkhw,bgkhw->bgnhw', patches, Kmap)
        return out.reshape(b, c, h, w)

    def _L1_attn_ref(x, att_w, z_w, z_b, r_w, r_b, f_w, f_b):
        import jax, jax.numpy as jnp
        import numpy as np
        F_DIM = 64
        F = x.shape[-1]
        wa, wb, wc = (att_w[:F], att_w[F:2 * F], att_w[2 * F:])
        a = jnp.einsum('bif,f->bi', x, wa)
        b = jnp.einsum('bjf,f->bj', x, wb)
        c = jnp.einsum('bif,bjf->bij', x * wc, x)
        scores = a[:, :, None] + b[:, None, :] + c
        attn_weight = jax.nn.softmax(scores, axis=2)
        attn = jnp.einsum('bij,bjf->bif', attn_weight, x)
        cat = jnp.concatenate([x, attn], axis=-1)
        z = jnp.tanh(jnp.einsum('bsg,fg->bsf', cat, z_w) + z_b)
        r = jax.nn.sigmoid(jnp.einsum('bsg,fg->bsf', cat, r_w) + r_b)
        f = jax.nn.sigmoid(jnp.einsum('bsg,fg->bsf', cat, f_w) + f_b)
        return r * x + f * z

    def _L1_ffn_ref(x, router_w, w1, w2, w3):
        import jax, jax.numpy as jnp
        import numpy as np
        N_EXPERTS = 8
        TOP_K = 2
        B, T, C = x.shape
        flat = x.reshape(-1, C)
        logits = flat @ router_w.T
        probs = jax.nn.softmax(logits, axis=-1)
        topk_probs, topk_idx = jax.lax.top_k(probs, TOP_K)
        topk_probs = topk_probs / (jnp.sum(topk_probs, axis=-1, keepdims=True) + 1e-09)
        onehot = jax.nn.one_hot(topk_idx, N_EXPERTS, dtype=flat.dtype)
        gates = jnp.einsum('nk,nke->ne', topk_probs, onehot)
        h1 = jnp.einsum('nc,ehc->neh', flat, w1)
        h3 = jnp.einsum('nc,ehc->neh', flat, w3)
        h = jax.nn.silu(h1) * h3
        y = jnp.einsum('neh,ech->nec', h, w2)
        out = jnp.einsum('ne,nec->nc', gates, y)
        return out.reshape(B, T, C)

    def _gn(v, G=32, eps=1e-05):
        B_, C_, H_, W_ = v.shape
        g = v.reshape(B_, G, C_ // G, H_, W_)
        m = jnp.mean(g, axis=(2, 3, 4), keepdims=True)
        s = jnp.var(g, axis=(2, 3, 4), keepdims=True)
        return ((g - m) / jnp.sqrt(s + eps)).reshape(v.shape)

    def _ln_c(v, eps=1e-06):
        m = jnp.mean(v, axis=1, keepdims=True)
        s = jnp.var(v, axis=1, keepdims=True)
        return (v - m) / jnp.sqrt(s + eps)

    def _ln_t(v, eps=1e-05):
        m = jnp.mean(v, axis=-1, keepdims=True)
        s = jnp.var(v, axis=-1, keepdims=True)
        return (v - m) / jnp.sqrt(s + eps)

    def _to_tokens(v):
        B_, C_, H_, W_ = v.shape
        return v.reshape(B_, C_, H_ * W_).transpose(0, 2, 1)

    def _from_tokens(t, like):
        B_, C_, H_, W_ = like.shape
        return t.transpose(0, 2, 1).reshape(B_, C_, H_, W_)
    x = x + _L0_conv_ref(_gn(x), L0_conv_w_reduce, L0_conv_b_reduce, L0_conv_w_span, L0_conv_b_span)
    t = _to_tokens(x)
    t = t + _L1_attn_ref(_ln_t(t), L1_attn_att_w, L1_attn_z_w, L1_attn_z_b, L1_attn_r_w, L1_attn_r_b, L1_attn_f_w, L1_attn_f_b)
    t = t + _L1_ffn_ref(_ln_t(t), L1_ffn_router_w, L1_ffn_w1, L1_ffn_w2, L1_ffn_w3)
    x = _from_tokens(t, x)
    return x

_drawn_inputs = setup_inputs


def setup_inputs(seed=0):
    import zlib

    import numpy as np

    out = dict(_drawn_inputs(seed))
    spreads = {'L0_conv_b_reduce': (0.0, 0.1), 'L0_conv_b_span': (0.0, 0.1)}
    factors = {'L1_attn_z_b': 5.608, 'L1_attn_r_b': 8.0, 'L1_attn_f_b': 25.436}
    for name, (base, spread) in spreads.items():
        noise = np.random.default_rng([zlib.crc32(name.encode()), seed]).standard_normal(out[name].shape)
        drawn = base * np.exp(spread * noise) if base else spread * noise
        out[name] = jnp.asarray(drawn.astype(out[name].dtype))
    for name, factor in factors.items():
        out[name] = (out[name] * factor).astype(out[name].dtype)
    return out
```

```python
from contextlib import ExitStack

import numpy as np
import concourse.bass as bass
from concourse import mybir

F32 = mybir.dt.float32
F32R = mybir.dt.float32r
ALU = mybir.AluOpType
ACT = mybir.ActivationFunctionType
AX_X = mybir.AxisListType.X

P = 128
B, C, IMG = 8, 64, 16
PX = IMG * IMG
PAIRS = B // 2
TOK = 2 * PX
TILES = TOK // P
NTILES = PAIRS * TILES
HID = C // 4
TAPS, PADW = 9, IMG + 2
EXPERTS, HMOE = 8, 682
MAIN = HMOE // P
REST = HMOE - MAIN * P
TAILS = -(-REST * EXPERTS // P)
CHUNKS = MAIN * EXPERTS + TAILS
PIECES = 16
PIECE = 2 * CHUNKS * P // PIECES
STAGES = 4

PAIRAVG, WRED, BRED, IDENT = 0, P, 2 * P, 2 * P + 1
EARLY = IDENT + P
ATTS, ATTB, GATEW, GATEB, ROUTW, REV, FOLD = np.cumsum([0, 1, 1, 3 * C, 3 * C, EXPERTS, EXPERTS]) + EARLY
PACKED = int(FOLD) + C
ATTS, ATTB, GATEW, GATEB, ROUTW, REV, FOLD = map(int, (ATTS, ATTB, GATEW, GATEB, ROUTW, REV, FOLD))

EARLY_EXPERTS = 2
SEQ = [(e, m) for e in range(EARLY_EXPERTS) for m in range(MAIN)]
SEQ += [(None, q) for q in range(TAILS)]
SEQ += [(e, m) for e in range(EARLY_EXPERTS, EXPERTS) for m in range(MAIN)]
POS = {c: s for s, c in enumerate(SEQ)}
GATES = EXPERTS + TAILS
OUTS = EXPERTS + 1


def column(chunk):
    e, m = chunk
    return (EXPERTS * MAIN + m) if e is None else e * MAIN + m


def last_of(e):
    return POS[(e, MAIN - 1)]


TAIL_LAST = POS[(None, TAILS - 1)]
GATE_AT = {POS[(e, 0)] + 1: e for e in range(EXPERTS)}
GATE_AT.update({3 + 2 * q: EXPERTS + q for q in range(TAILS)})
GATE_ORDER = [GATE_AT[s] for s in sorted(GATE_AT)]
assert len(GATE_ORDER) == GATES
OUT_ORDER = sorted([(last_of(e), e) for e in range(EXPERTS)] + [(TAIL_LAST, EXPERTS)])


def build(nc, x, packed, wspan, w1, w3, w2, sel, out):
    with ExitStack() as ctx:
        def sb(name, shape, dt=F32):
            return ctx.enter_context(nc.sbuf_tensor(name, shape, dt))

        def sem(name):
            return ctx.enter_context(nc.semaphore(name))

        bank = [ctx.enter_context(nc.psum_tensor(f"bank{i}", [P, 512], F32)) for i in range(8)]

        par = sb("par", [P, PACKED])
        w13 = sb("w13", [P, 2 * CHUNKS * P], F32R)
        stage = sb("stage", [P, STAGES, PIECE])
        w2_sb = sb("w2_sb", [P, CHUNKS, C])
        sel_raw = sb("sel_raw", [P, GATES * P])
        sel_sb = sb("sel_sb", [P, GATES * P], F32R)
        ident = par[:, IDENT:IDENT + P]
        x_hl = sb("x_hl", [P, PAIRS * TOK], F32R)
        x_lh = sb("x_lh", [P, PAIRS * TOK], F32R)
        gT = sb("gT", [P, PAIRS * TOK], F32R)
        acc = sb("acc", [P, PAIRS * TOK])
        minus_half = sb("minus_half", [P, TILES])

        before = ExitStack()

        def sb(name, shape, dt=F32):
            return before.enter_context(nc.sbuf_tensor(name, shape, dt))
        t_tok = sb("t_tok", [P, NTILES, C])
        ln_st = sb("ln_st", [P, NTILES, 6])
        ln_mv = sb("ln_mv", [P, NTILES, 2])
        ln_ve = sb("ln_ve", [P, NTILES])
        ln_rs = sb("ln_rs", [P, NTILES])
        n1 = sb("n1", [P, NTILES, 2, C])
        kT = sb("kT", [P, PAIRS * TOK])
        t2 = sb("t2", [P, NTILES, 2 * C])
        ln2_st = sb("ln2_st", [P, NTILES, 6])
        ln2_mv = sb("ln2_mv", [P, NTILES, 2])
        ln2_ve = sb("ln2_ve", [P, NTILES])
        ln2_rs = sb("ln2_rs", [P, NTILES])
        n2 = sb("n2", [P, 2, TILES, C])
        hlh = sb("hlh", [P, 2, TILES, 3 * C])
        rt = sb("rt", [P, 12, TILES, EXPERTS])
        rs = sb("rs", [P, 10, TILES])
        gsplit = sb("gsplit", [P, 2, TILES, P])

        involution = ExitStack()

        def sb(name, shape, dt=F32):
            return involution.enter_context(nc.sbuf_tensor(name, shape, dt))
        wspan_sb = sb("wspan_sb", [P, TAPS * P])
        xin = sb("xin", [P, PAIRS, PX])
        xpad = sb("xpad", [P, PAIRS, PADW, PADW])
        gn_st = sb("gn_st", [P, PAIRS, 6])
        gn_mv = sb("gn_mv", [P, PAIRS, 2])
        gn_avg = sb("gn_avg", [P, PAIRS, 2])
        gn_d = sb("gn_d", [P, PAIRS])
        gn_d2 = sb("gn_d2", [P, PAIRS])
        gn_var = sb("gn_var", [P, PAIRS])
        gn_rstd = sb("gn_rstd", [P, PAIRS])
        gn_bias = sb("gn_bias", [P, PAIRS])
        hid = sb("hid", [P, 2, TOK])
        prod = sb("prod", [P, TAPS, TOK])
        acc_p = sb("acc_p", [P, TOK])
        acc_v = sb("acc_v", [P, TOK])
        tcm = sb("tcm", [P, PAIRS, PX])
        involution.close()

        def sb(name, shape, dt=F32):
            return before.enter_context(nc.sbuf_tensor(name, shape, dt))
        qT = sb("qT", [P, PAIRS * TOK])
        cat = sb("cat", [P, PAIRS * TOK])
        mx = sb("mx", [P, B, 2])
        nmx = sb("nmx", [P, B, 2])
        ssum = sb("ssum", [P, B, 2])
        rsum = sb("rsum", [P, B, 2])
        prob = sb("prob", [P, 2, 2, PX])
        probT = sb("probT", [P, 2, 2, PX])
        zrf = sb("zrf", [P, 2, TILES, 3 * C])
        zrft = sb("zrft", [P, 2, TILES, 3 * C])
        gu = sb("gu", [P, TILES, C])
        gv = sb("gv", [P, TILES, C])
        gw = sb("gw", [P, TILES, C])
        before.close()

        def sb(name, shape, dt=F32):
            return ctx.enter_context(nc.sbuf_tensor(name, shape, dt))
        silu = sb("silu", [P, 4, TOK])
        hbuf = sb("hbuf", [P, 4, TOK])
        htail = sb("htail", [P, TAILS, TOK])
        gbc = sb("gbc", [P, GATES, TOK])
        ysc = sb("ysc", [P, TOK])
        y_out = sb("y_out", [C, PAIRS, TOK])

        (x_in, early_in, span_in, late_in, w2_in, sel_in) = map(
            sem, ("x_in", "early_in", "span_in", "late_in", "w2_in", "sel_in"))
        stage_in = [sem(f"stage_in{i}") for i in range(STAGES)]
        x_ins = [sem(f"x_in{i}") for i in range(PAIRS)]
        names = """pads_zero span_zero sel_zero consts_set gn_stats gn_means gn_avg_ready gn_avg_sb gn_d_ready gn_d2_ready
        gn_var_ready gn_rstd_ready gn_bias_ready xn_ready hidp_ready hid_ready kmap_ready prod_ready pool_add
        vec_add t_ready tT_ready t_tok_ready ln_st_ready ln_mv_ready ln_ve_ready ln_rs_ready n1_ready n1T_ready
        q_ready k_ready cat_x scores_ready mx_ready nmx_ready exp_ready rsum_ready prob_ready probT_ready
        probT_sb attn_ready cat_attn gates_ready zrf_ready tanh_ready gu_ready gv_ready gw_ready t2_ready
        ln2_st_ready ln2_mv_ready ln2_ve_ready ln2_rs_ready n2_ready hi_ready lo_ready hl_ready lh_ready t2T_ready
        hl_sb lh_sb acc_init logits_ready shifted_ready rexp_ready rchain gsplit_ready gT_ready gT_sb
        w_high w_split sel_ready
        up_ready silu_ready h_ready tail_gated down_done gb_ready gb_sb out_scaled out_added
        fold_ready y_ready stored""".split()
        S = {n: sem(n) for n in names}

        block = ctx.enter_context(nc.Block())

        def tiles(p):
            return slice(p * TILES, (p + 1) * TILES)

        def toks(p):
            return slice(p * TOK, (p + 1) * TOK)

        @block.sync
        def _(sp):
            for p in range(PAIRS):
                sp.dma_start(xin[:, p, :], x[2 * p:2 * p + 2].rearrange("b c s -> (b c) s")).then_inc(x_ins[p], 16)
            sp.dma_start(par[:, 0:EARLY], packed[:, 0:EARLY]).then_inc(early_in, 16)
            sp.wait_ge(S["span_zero"], 1)
            sp.dma_start(wspan_sb[0:2 * HID + 1, :], wspan).then_inc(span_in, 16)
            sp.dma_start(par[:, EARLY:PACKED], packed[:, EARLY:PACKED]).then_inc(late_in, 16)
            sp.wait_ge(S["sel_zero"], 1)
            sp.dma_start(sel_raw[0:2 * EXPERTS, :], sel).then_inc(sel_in, 16)
            for i in range(PIECES):
                if i >= STAGES:
                    sp.wait_ge(S["w_split"], i - STAGES + 1)
                src = (w1 if i < PIECES // 2 else w3)[:, bass.ts(i % (PIECES // 2), PIECE)]
                for h in range(2):
                    sp.dma_start(stage[h * C:(h + 1) * C, i % STAGES, :], src).then_inc(stage_in[i % STAGES], 16)
                if i == STAGES:
                    sp.dma_start(w2_sb[:], w2.rearrange("p (k c) -> p k c", c=C)).then_inc(w2_in, 16)
            for p in range(PAIRS):
                sp.wait_ge(S["y_ready"], p + 1)
                sp.dma_start(out[2 * p:2 * p + 2].rearrange("b c s -> c b s"),
                             y_out[:, p, :].rearrange("c (b s) -> c b s", b=2)).then_inc(S["stored"], 16)
            sp.wait_ge(S["stored"], 16 * PAIRS)

        @block.gpsimd
        def _(pool):
            g = nc.gpsimd
            g.memset(minus_half[:], -0.5).then_inc(S["consts_set"], 1)
            g.memset(sel_raw[:], 0.0).then_inc(S["sel_zero"], 1)
            g.memset(t2[:, :, C:2 * C], 0.0).then_inc(S["consts_set"], 1)
            g.memset(gsplit[:, :, :, 2 * EXPERTS:P], 0.0).then_inc(S["consts_set"], 1)
            pool.wait_ge(S["consts_set"], 3)
            g.memset(kT[C:P, :], 1.0).then_inc(S["consts_set"], 1)
            pool.wait_ge(S["consts_set"], 4)
            pool.wait_ge(S["gn_var_ready"], 1)
            g.tensor_tensor(gn_rstd[:], gn_var[:], minus_half[:], ALU.pow).then_inc(S["gn_rstd_ready"], 1)
            adds = 0
            for q in range(2):
                for i, k in enumerate((0, 1, 2, 4, 6)):
                    pool.wait_ge(S["prod_ready"], q * TAPS + k + 1)
                    if i:
                        pool.wait_ge(S["pool_add"], adds)
                        src = acc_p[:]
                    else:
                        if q:
                            pool.wait_ge(S["t_ready"], q)
                        src = xin[:, 2 * q:2 * q + 2, :].rearrange("p a s -> p (a s)")
                    g.tensor_tensor(acc_p[:], src, prod[:, k, :], ALU.add).then_inc(S["pool_add"], 1)
                    adds += 1
            done = 0

            def split(n):
                nonlocal done
                for i in range(done, done + n):
                    pool.wait_ge(S["w_high"], i + 1)
                    g.tensor_tensor(w13[C:P, bass.ts(i, PIECE)], stage[C:P, i % STAGES, :],
                                    w13[C:P, bass.ts(i, PIECE)].bitcast(F32), ALU.subtract).then_inc(S["w_split"], 1)
                done += n
            for s in range(PAIRS + 1):
                if s < PAIRS:
                    pool.wait_ge(S["ln_ve_ready"], s + 1)
                    if done:
                        pool.wait_ge(S["w_split"], done)
                    g.tensor_tensor(ln_rs[:, tiles(s)], ln_ve[:, tiles(s)], minus_half[:], ALU.pow).then_inc(S["ln_rs_ready"], 1)
                    pool.wait_ge(S["ln_rs_ready"], s + 1)
                    split(2)
                if s:
                    pool.wait_ge(S["ln2_ve_ready"], s)
                    pool.wait_ge(S["w_split"], done)
                    g.tensor_tensor(ln2_rs[:, tiles(s - 1)], ln2_ve[:, tiles(s - 1)], minus_half[:], ALU.pow).then_inc(S["ln2_rs_ready"], 1)
                    pool.wait_ge(S["ln2_rs_ready"], s)
                    split(2)
            assert done == PIECES
            pool.wait_ge(S["w_split"], PIECES)
            with pool.Fori(0, PAIRS) as tb:
                for m in range(TAILS):
                    s = POS[(None, m)]
                    pool.wait_ge(S["h_ready"], tb * CHUNKS + s + 1)
                    pool.wait_ge(S["gb_sb"], tb * GATES + GATE_ORDER.index(EXPERTS + m) + 1)
                    g.tensor_tensor(htail[:, m, :], hbuf[:, s % 4, :], gbc[:, EXPERTS + m, :],
                                    ALU.mult).then_inc(S["tail_gated"], 1)

        @block.scalar
        def _(act):
            a = nc.scalar
            for q in range(2):
                act.wait_ge(S["hidp_ready"], q + 1)
                a.activation(hid[:, q, :], bank[5 + q][:], ACT.Relu, bias=par[:, BRED:BRED + 1]).then_inc(S["hid_ready"], 1)
            for q in range(2):
                act.wait_ge(S["tT_ready"], q + 1)
                for r in range(2):
                    p = 2 * q + r
                    a.copy(t_tok[:, tiles(p), :].rearrange("p (b h) c -> p h b c", b=2),
                           bank[4 * q][:, r * PX:(r + 1) * PX].rearrange("p (h b c) -> p h b c", h=2, b=2)).then_inc(S["t_tok_ready"], 1)
            act.wait_ge(sel_in, 16)
            a.copy(sel_sb[:], sel_raw[:]).then_inc(S["sel_ready"], 1)
            done = 0

            def high(n):
                nonlocal done
                for i in range(done, done + n):
                    act.wait_ge(stage_in[i % STAGES], 32 * (i // STAGES + 1))
                    a.copy(w13[:, bass.ts(i, PIECE)], stage[:, i % STAGES, :]).then_inc(S["w_high"], 1)
                done += n

            for s in range(PAIRS + 1):
                if s < PAIRS:
                    p = s
                    act.wait_ge(S["n1T_ready"], p + 1)
                    act.wait_ge(S["consts_set"], 4)
                    act.wait_ge(S["q_ready"], p + 1)
                    a.copy(kT[0:C, toks(p)], bank[0][0:C, :]).then_inc(S["k_ready"], 1)
                    a.copy(cat[0:C, toks(p)], bank[0][0:C, :]).then_inc(S["cat_x"], 1)
                    high(2)
                    for r in range(2):
                        b = 2 * p + r
                        act.wait_ge(S["nmx_ready"], b + 1)
                        if b >= 2:
                            act.wait_ge(S["probT_ready"], b - 1)
                        for i in range(2):
                            a.activation(prob[:, r, i, :], bank[1 + r][:, i * PX:(i + 1) * PX], ACT.Exp,
                                         bias=nmx[:, b, i:i + 1], accum_out=ssum[:, b, i:i + 1]).then_inc(S["exp_ready"], 1)
                    for r in range(2):
                        b = 2 * p + r
                        act.wait_ge(S["probT_ready"], b + 1)
                        if b >= 2:
                            act.wait_ge(S["attn_ready"], b - 1)
                        a.copy(probT[:, r].rearrange("p j i -> p (j i)"), bank[3][:]).then_inc(S["probT_sb"], 1)
                    act.wait_ge(S["attn_ready"], 2 * p + 2)
                    a.copy(cat[C:P, toks(p)], bank[4][C:P, :]).then_inc(S["cat_attn"], 1)
                    act.wait_ge(S["zrf_ready"], 2 * p + 2)
                    if p >= 2:
                        act.wait_ge(S["gv_ready"], p - 1)
                    a.activation(zrft[:, p % 2, :, 0:C], zrf[:, p % 2, :, 0:C], ACT.Tanh).then_inc(S["tanh_ready"], 1)
                    a.activation(zrft[:, p % 2, :, C:3 * C], zrf[:, p % 2, :, C:3 * C], ACT.Tanh, scale=0.5).then_inc(S["tanh_ready"], 1)
                if s:
                    p = s - 1
                    high(2)
                    act.wait_ge(S["hl_ready"], p + 1)
                    a.copy(x_hl[:, toks(p)], bank[7][:]).then_inc(S["hl_sb"], 1)
                    act.wait_ge(S["lh_ready"], p + 1)
                    a.copy(x_lh[:, toks(p)], bank[4][:]).then_inc(S["lh_sb"], 1)
                    act.wait_ge(S["shifted_ready"], p + 1)
                    a.activation(rt[:, 1], rt[:, 0], ACT.Exp).then_inc(S["rexp_ready"], 1)
                    act.wait_ge(S["gT_ready"], p + 1)
                    a.copy(gT[:, toks(p)], bank[7][:]).then_inc(S["gT_sb"], 1)
            assert done == PIECES
            with act.Fori(0, PAIRS) as tb:
                for s in range(CHUNKS):
                    act.wait_ge(S["up_ready"], tb * 2 * CHUNKS + 2 * s + 1)
                    act.wait_ge(S["h_ready"], tb * CHUNKS + max(s - 3, 0))
                    a.activation(silu[:, s % 4, :], bank[s % 2][:], ACT.Silu).then_inc(S["silu_ready"], 1)
                    if s in GATE_AT:
                        i = GATE_AT[s]
                        act.wait_ge(S["gb_ready"], tb * GATES + GATE_ORDER.index(i) + 1)
                        if i < EXPERTS:
                            act.wait_ge(S["out_added"], tb * OUTS)
                        else:
                            act.wait_ge(S["tail_gated"], tb * TAILS)
                        a.copy(gbc[:, i, :], bank[7][:]).then_inc(S["gb_sb"], 1)
            for p in range(PAIRS):
                act.wait_ge(S["fold_ready"], p + 1)
                a.copy(y_out[:, p, :], bank[p % 2][0:C, :]).then_inc(S["y_ready"], 1)

        @block.vector
        def _(dve):
            v = nc.vector
            v.memset(wspan_sb[:], 0.0).then_inc(S["span_zero"], 1)
            v.memset(xpad[:].rearrange("p a y x -> p (a y x)"), 0.0).then_inc(S["pads_zero"], 1)
            for p in range(PAIRS):
                dve.wait_ge(x_ins[p], 16)
                v.bn_stats(gn_st[:, p], xin[:, p, :]).then_inc(S["gn_stats"], 1)
            for p in range(PAIRS):
                dve.wait_ge(S["gn_stats"], p + 1)
                v.bn_aggr(gn_mv[:, p], gn_st[:, p]).then_inc(S["gn_means"], 1)
            dve.wait_ge(S["gn_avg_ready"], 1)
            v.tensor_copy(gn_avg[:].rearrange("p a b -> p (a b)"), bank[0][:, 0:2 * PAIRS]).then_inc(S["gn_avg_sb"], 1)
            dve.wait_ge(S["gn_avg_sb"], 1)
            v.tensor_tensor(gn_d[:], gn_mv[:, :, 0], gn_avg[:, :, 0], ALU.subtract).then_inc(S["gn_d_ready"], 1)
            dve.wait_ge(S["gn_d_ready"], 1)
            v.tensor_tensor(gn_d2[:], gn_d[:], gn_d[:], ALU.mult).then_inc(S["gn_d2_ready"], 1)
            dve.wait_ge(S["gn_d2_ready"], 1)
            v.scalar_tensor_tensor(gn_var[:], gn_d2[:], 1e-5, gn_avg[:, :, 1], ALU.add, ALU.add).then_inc(S["gn_var_ready"], 1)
            dve.wait_ge(S["gn_rstd_ready"], 1)
            v.scalar_tensor_tensor(gn_bias[:], gn_avg[:, :, 0], -1.0, gn_rstd[:], ALU.mult, ALU.mult).then_inc(S["gn_bias_ready"], 1)
            dve.wait_ge(S["gn_bias_ready"], 1)
            dve.wait_ge(S["pads_zero"], 1)
            for p in range(PAIRS):
                v.tensor_scalar(xpad[:, p, 1:1 + IMG, 1:1 + IMG], xin[:, p, :].rearrange("p (y x) -> p y x", y=IMG),
                                gn_rstd[:, p:p + 1], gn_bias[:, p:p + 1], ALU.mult, ALU.add).then_inc(S["xn_ready"], 1)
            dve.wait_ge(S["xn_ready"], PAIRS)
            adds = 0
            n = 0
            for q in range(2):
                for k in range(TAPS):
                    if q:
                        dve.wait_ge(S["pool_add"], 5)
                    dve.wait_ge(S["kmap_ready"], n + 1)
                    v.tensor_tensor(prod[:, k, :].rearrange("p (a y x) -> p a y x", a=2, y=IMG),
                                    bank[1 + n % 3][:].rearrange("p (a y x) -> p a y x", a=2, y=IMG),
                                    xpad[:, 2 * q:2 * q + 2, k // 3:k // 3 + IMG, k % 3:k % 3 + IMG],
                                    ALU.mult).then_inc(S["prod_ready"], 1)
                    n += 1
                    if k in (5, 7, 8):
                        first, second = (prod[:, 3, :], prod[:, 5, :]) if k == 5 else (acc_v[:], prod[:, k, :])
                        dve.wait_ge(S["prod_ready"], n)
                        if adds:
                            dve.wait_ge(S["vec_add"], adds)
                        v.tensor_tensor(acc_v[:], first, second, ALU.add).then_inc(S["vec_add"], 1)
                        adds += 1
                dve.wait_ge(S["vec_add"], adds)
                dve.wait_ge(S["pool_add"], 5 * (q + 1))
                v.tensor_tensor(tcm[:, 2 * q:2 * q + 2, :].rearrange("p a s -> p (a s)"), acc_v[:], acc_p[:],
                                ALU.add).then_inc(S["t_ready"], 1)

            def norm_stats(p, src, st, mv, ve, eps_sems):
                st_s, mv_s, ve_s = (S[n] for n in eps_sems)
                for i in range(TILES):
                    v.bn_stats(st[:, p * TILES + i], src[:, p * TILES + i, 0:C]).then_inc(st_s, 1)
                for i in range(TILES):
                    dve.wait_ge(st_s, p * TILES + i + 1)
                    v.bn_aggr(mv[:, p * TILES + i], st[:, p * TILES + i]).then_inc(mv_s, 1)
                dve.wait_ge(mv_s, (p + 1) * TILES)
                v.tensor_scalar_add(ve[:, tiles(p)], mv[:, tiles(p), 1], 1e-5).then_inc(ve_s, 1)

            chain = [0]

            def link(ins):
                chain[0] += 1
                ins.then_inc(S["rchain"], 1)
                dve.wait_ge(S["rchain"], chain[0])

            for s in range(PAIRS + 1):
                if s < PAIRS:
                    p = s
                    dve.wait_ge(S["t_tok_ready"], p + 1)
                    norm_stats(p, t_tok, ln_st, ln_mv, ln_ve, ("ln_st_ready", "ln_mv_ready", "ln_ve_ready"))
                    dve.wait_ge(S["ln_rs_ready"], p + 1)
                    for i in range(TILES):
                        t = p * TILES + i
                        v.tensor_scalar(n1[:, t], t_tok[:, t:t + 1, :].to_broadcast([P, 2, C]), ln_mv[:, t, 0:1],
                                        ln_rs[:, t:t + 1], ALU.subtract, ALU.mult).then_inc(S["n1_ready"], 1)
                    dve.wait_ge(S["n1T_ready"], p + 1)
                    if p == 0:
                        dve.wait_ge(late_in, 16)
                    v.tensor_scalar(qT[:, toks(p)], bank[0][:], par[:, ATTS:ATTS + 1], par[:, ATTB:ATTB + 1],
                                    ALU.mult, ALU.add).then_inc(S["q_ready"], 1)
                    for r in range(2):
                        b = 2 * p + r
                        dve.wait_ge(S["scores_ready"], b + 1)
                        v.tensor_reduce(mx[:, b], bank[1 + r][:].rearrange("p (i j) -> p i j", i=2), AX_X, ALU.max).then_inc(S["mx_ready"], 1)
                        dve.wait_ge(S["mx_ready"], b + 1)
                        v.tensor_scalar_mul(nmx[:, b], mx[:, b], -1.0).then_inc(S["nmx_ready"], 1)
                    for r in range(2):
                        b = 2 * p + r
                        dve.wait_ge(S["exp_ready"], 2 * b + 2)
                        v.reciprocal(rsum[:, b], ssum[:, b]).then_inc(S["rsum_ready"], 1)
                        dve.wait_ge(S["rsum_ready"], b + 1)
                        for i in range(2):
                            v.tensor_scalar_mul(prob[:, r, i, :], prob[:, r, i, :], rsum[:, b, i:i + 1]).then_inc(S["prob_ready"], 1)
                    for h in range(2):
                        dve.wait_ge(S["gates_ready"], 2 * p + h + 1)
                        if p >= 2:
                            dve.wait_ge(S["tanh_ready"], 2 * (p - 1))
                        v.tensor_tensor(zrf[:, p % 2, 2 * h:2 * h + 2, :],
                                        bank[5 + h][:, 0:6 * C].rearrange("p (t c) -> p t c", t=2),
                                        par[:, GATEB:GATEB + 3 * C].rearrange("p (t c) -> p t c", t=1).to_broadcast([P, 2, 3 * C]),
                                        ALU.add).then_inc(S["zrf_ready"], 1)
                    dve.wait_ge(S["tanh_ready"], 2 * p + 2)
                    zt = zrft[:, p % 2]
                    v.scalar_tensor_tensor(gu[:], zt[:, :, C:2 * C], 1.0, n1[:, tiles(p), 0, :], ALU.add, ALU.mult).then_inc(S["gu_ready"], 1)
                    v.scalar_tensor_tensor(gv[:], zt[:, :, 2 * C:3 * C], 1.0, zt[:, :, 0:C], ALU.add, ALU.mult).then_inc(S["gv_ready"], 1)
                    dve.wait_ge(S["gu_ready"], p + 1)
                    dve.wait_ge(S["gv_ready"], p + 1)
                    v.tensor_tensor(gw[:], gu[:], gv[:], ALU.add).then_inc(S["gw_ready"], 1)
                    dve.wait_ge(S["gw_ready"], p + 1)
                    v.scalar_tensor_tensor(t2[:, tiles(p), 0:C], gw[:], 0.5, t_tok[:, tiles(p), :], ALU.mult, ALU.add).then_inc(S["t2_ready"], 1)
                    dve.wait_ge(S["t2_ready"], p + 1)
                    norm_stats(p, t2, ln2_st, ln2_mv, ln2_ve, ("ln2_st_ready", "ln2_mv_ready", "ln2_ve_ready"))
                if s:
                    p = s - 1
                    k = p % 2
                    dve.wait_ge(S["ln2_rs_ready"], p + 1)
                    for i in range(TILES):
                        t = p * TILES + i
                        v.tensor_scalar(n2[:, k, i, :], t2[:, t, 0:C], ln2_mv[:, t, 0:1],
                                        ln2_rs[:, t:t + 1], ALU.subtract, ALU.mult).then_inc(S["n2_ready"], 1)
                    dve.wait_ge(S["n2_ready"], (p + 1) * TILES)
                    if p >= 2:
                        dve.wait_ge(S["lh_ready"], p - 1)
                    hi = hlh[:, k].bitcast(F32R)
                    v.tensor_copy(hi[:, :, 0:C], n2[:, k]).then_inc(S["hi_ready"], 1)
                    v.tensor_copy(hi[:, :, 2 * C:3 * C], n2[:, k]).then_inc(S["hi_ready"], 1)
                    dve.wait_ge(S["hi_ready"], 2 * p + 2)
                    v.tensor_tensor(hlh[:, k, :, C:2 * C], n2[:, k], hlh[:, k, :, 0:C], ALU.subtract).then_inc(S["lo_ready"], 1)
                    dve.wait_ge(S["t2T_ready"], p + 1)
                    v.tensor_copy(acc[:, toks(p)], bank[5][:]).then_inc(S["acc_init"], 1)
                    dve.wait_ge(S["logits_ready"], p + 1)

                    def wide(i):
                        return rs[:, i].rearrange("p (t e) -> p t e", e=1).to_broadcast([P, TILES, EXPERTS])
                    logits = bank[6][:, 0:TILES * EXPERTS].rearrange("p (t e) -> p t e", e=EXPERTS)
                    rev = par[:, REV:REV + EXPERTS].rearrange("p (t e) -> p t e", t=1).to_broadcast([P, TILES, EXPERTS])
                    link(v.tensor_reduce(rs[:, 0], logits, AX_X, ALU.max))
                    v.tensor_tensor(rt[:, 0], logits, wide(0), ALU.subtract).then_inc(S["shifted_ready"], 1)
                    dve.wait_ge(S["rexp_ready"], p + 1)
                    link(v.tensor_reduce(rs[:, 1], rt[:, 1], AX_X, ALU.add))
                    link(v.reciprocal(rs[:, 2], rs[:, 1]))
                    link(v.tensor_tensor(rt[:, 2], rt[:, 1], wide(2), ALU.mult))
                    link(v.tensor_reduce(rs[:, 3], rt[:, 2], AX_X, ALU.max))
                    link(v.tensor_tensor(rt[:, 3], rt[:, 2], wide(3), ALU.is_ge))
                    link(v.tensor_tensor(rt[:, 4], rt[:, 3], rev, ALU.mult))
                    link(v.tensor_reduce(rs[:, 4], rt[:, 4], AX_X, ALU.max))
                    link(v.tensor_tensor(rt[:, 5], rt[:, 4], wide(4), ALU.is_equal))
                    link(v.scalar_tensor_tensor(rt[:, 6], rt[:, 5], -2.0, rt[:, 2], ALU.mult, ALU.add))
                    link(v.tensor_reduce(rs[:, 5], rt[:, 6], AX_X, ALU.max))
                    link(v.tensor_tensor(rt[:, 7], rt[:, 6], wide(5), ALU.is_ge))
                    link(v.tensor_tensor(rt[:, 8], rt[:, 7], rev, ALU.mult))
                    link(v.tensor_reduce(rs[:, 6], rt[:, 8], AX_X, ALU.max))
                    link(v.tensor_tensor(rt[:, 9], rt[:, 8], wide(6), ALU.is_equal))
                    link(v.tensor_tensor(rt[:, 10], rt[:, 5], rt[:, 9], ALU.add))
                    link(v.scalar_tensor_tensor(rs[:, 7], rs[:, 3], 1e-9, rs[:, 5], ALU.add, ALU.add))
                    link(v.reciprocal(rs[:, 8], rs[:, 7]))
                    link(v.tensor_tensor(rt[:, 11], rt[:, 10], rt[:, 2], ALU.mult))
                    link(v.tensor_tensor(rt[:, 3], rt[:, 11], wide(8), ALU.mult))
                    if p >= 2:
                        dve.wait_ge(S["gT_ready"], p - 1)
                    link(v.tensor_copy(gsplit[:, k].bitcast(F32R)[:, :, 0:EXPERTS], rt[:, 3]))
                    v.tensor_tensor(gsplit[:, k, :, EXPERTS:2 * EXPERTS], rt[:, 3], gsplit[:, k, :, 0:EXPERTS],
                                    ALU.subtract).then_inc(S["gsplit_ready"], 1)
            with dve.Fori(0, PAIRS) as tb:
                outs = list(OUT_ORDER)
                n_out = 0
                here = bass.ds(tb * TOK, TOK)

                def take_out(n_out, last, e):
                    slot = e % 2 if e < EXPERTS else 2
                    dve.wait_ge(S["down_done"], tb * CHUNKS + last + 1)
                    if e < EXPERTS:
                        dve.wait_ge(S["gb_sb"], tb * GATES + GATE_ORDER.index(e) + 1)
                        dve.wait_ge(S["out_added"], tb * OUTS + n_out)
                        v.tensor_tensor(ysc[:], bank[4 + slot][:], gbc[:, e, :], ALU.mult).then_inc(S["out_scaled"], 1)
                        dve.wait_ge(S["out_scaled"], tb * EXPERTS + sum(o[1] < EXPERTS for o in OUT_ORDER[:n_out + 1]))
                        v.tensor_tensor(acc[:, here], acc[:, here], ysc[:], ALU.add).then_inc(S["out_added"], 1)
                    else:
                        dve.wait_ge(S["out_added"], tb * OUTS + n_out)
                        v.tensor_tensor(acc[:, here], acc[:, here], bank[4 + slot][:], ALU.add).then_inc(S["out_added"], 1)
                for s in range(CHUNKS):
                    dve.wait_ge(S["silu_ready"], tb * CHUNKS + s + 1)
                    dve.wait_ge(S["up_ready"], tb * 2 * CHUNKS + 2 * s + 2)
                    dve.wait_ge(S["down_done"], tb * CHUNKS + max(s - 3, 0))
                    v.tensor_tensor(hbuf[:, s % 4, :], silu[:, s % 4, :], bank[2 + s % 2][:], ALU.mult).then_inc(S["h_ready"], 1)
                    if outs and 2 * (outs[0][0] // 2) + 3 <= s:
                        last, e = outs.pop(0)
                        take_out(n_out, last, e)
                        n_out += 1
                for last, e in outs:
                    take_out(n_out, last, e)
                    n_out += 1

        @block.tensor
        def _(pe):
            t = nc.tensor
            pe.wait_ge(early_in, 16)
            pe.wait_ge(S["gn_means"], PAIRS)
            t.matmul(bank[0][:, 0:2 * PAIRS], par[:, PAIRAVG:PAIRAVG + P], gn_mv[:].rearrange("p a b -> p (a b)"),
                     start=True, stop=True).then_inc(S["gn_avg_ready"], 1)
            pe.wait_ge(span_in, 16)
            pe.wait_ge(S["xn_ready"], PAIRS)
            for q in range(2):
                t.matmul(bank[5 + q][:], par[:, WRED:WRED + P], xpad[:, 2 * q:2 * q + 2, 1:1 + IMG, 1:1 + IMG],
                         start=True, stop=True).then_inc(S["hidp_ready"], 1)
            n = 0
            for q in range(2):
                pe.wait_ge(S["hid_ready"], q + 1)
                for k in range(TAPS):
                    if n >= 3:
                        pe.wait_ge(S["prod_ready"], n - 2)
                    t.matmul(bank[1 + n % 3][:], wspan_sb[:, bass.ts(k, P)], hid[:, q, :],
                             start=True, stop=True).then_inc(S["kmap_ready"], 1)
                    n += 1
            for q in range(2):
                pe.wait_ge(S["t_ready"], q + 1)
                for i in range(4):
                    last = t.transpose(bank[4 * q][:, bass.ts(i, P)], tcm[:, 2 * q + i // 2, bass.ts(i % 2, P)], ident)
                last.then_inc(S["tT_ready"], 1)
            pe.wait_ge(late_in, 16)
            pe.wait_ge(S["consts_set"], 4)
            pe.wait_ge(S["t_tok_ready"], PAIRS)
            for s in range(PAIRS + 1):
                if s < PAIRS:
                    p = s
                    pe.wait_ge(S["n1_ready"], (p + 1) * TILES)
                    if p:
                        pe.wait_ge(S["cat_x"], p)
                    for i in range(TILES):
                        last = t.transpose(bank[0][:, bass.ts(i, P)], n1[:, p * TILES + i].rearrange("p a c -> p (a c)"), ident)
                    last.then_inc(S["n1T_ready"], 1)
                    pe.wait_ge(S["q_ready"], p + 1)
                    pe.wait_ge(S["k_ready"], p + 1)
                    for r in range(2):
                        b = 2 * p + r
                        if b >= 2:
                            pe.wait_ge(S["exp_ready"], 2 * (b - 1))
                        for i in range(2):
                            last = t.matmul(bank[1 + r][:, i * PX:(i + 1) * PX], qT[:, b * PX + i * P:b * PX + (i + 1) * P],
                                            kT[:, b * PX:(b + 1) * PX], start=True, stop=True)
                        last.then_inc(S["scores_ready"], 1)
                    for r in range(2):
                        b = 2 * p + r
                        pe.wait_ge(S["prob_ready"], 2 * b + 2)
                        if b:
                            pe.wait_ge(S["probT_sb"], b)
                        for j in range(2):
                            for i in range(2):
                                last = t.transpose(bank[3][:, j * PX + i * P:j * PX + (i + 1) * P],
                                                   prob[:, r, i, bass.ts(j, P)], ident)
                        last.then_inc(S["probT_ready"], 1)
                        pe.wait_ge(S["probT_sb"], b + 1)
                        if r == 0 and p:
                            pe.wait_ge(S["cat_attn"], p)
                            if p >= 2:
                                pe.wait_ge(S["lh_sb"], p - 1)
                        for j in range(2):
                            last = t.matmul(bank[4][C:P, r * PX:(r + 1) * PX], n1[:, b * 2 + j, 0, :], probT[:, r, j, :],
                                            start=j == 0, stop=j == 1)
                        last.then_inc(S["attn_ready"], 1)
                    pe.wait_ge(S["cat_attn"], p + 1)
                    pe.wait_ge(S["cat_x"], p + 1)
                    for h in range(2):
                        if p:
                            pe.wait_ge(S["zrf_ready"], 2 * (p - 1) + h + 1)
                        if p >= 2:
                            pe.wait_ge(S["acc_init"] if h == 0 else S["shifted_ready"], p - 1)
                        for i in range(2):
                            k = p * TOK + (2 * h + i) * P
                            last = t.matmul(bank[5 + h][:, i * 3 * C:(i + 1) * 3 * C], cat[:, k:k + P],
                                            par[:, GATEW:GATEW + 3 * C], start=True, stop=True)
                        last.then_inc(S["gates_ready"], 1)
                if s:
                    p = s - 1
                    k = p % 2
                    pe.wait_ge(S["t2_ready"], p + 1)
                    pe.wait_ge(S["zrf_ready"], 2 * min(s + 1, PAIRS))
                    for i in range(TILES):
                        last = t.transpose(bank[5][:, bass.ts(i, P)], t2[:, p * TILES + i, :], ident)
                    last.then_inc(S["t2T_ready"], 1)
                    pe.wait_ge(S["lo_ready"], p + 1)
                    if p:
                        pe.wait_ge(S["gT_sb"], p)
                    for i in range(TILES):
                        last = t.transpose(bank[7][:, bass.ts(i, P)], hlh[:, k, i, 0:P], ident)
                    last.then_inc(S["hl_ready"], 1)
                    pe.wait_ge(S["cat_attn"], min(s + 1, PAIRS))
                    for i in range(TILES):
                        last = t.transpose(bank[4][:, bass.ts(i, P)], hlh[:, k, i, C:C + P], ident)
                    last.then_inc(S["lh_ready"], 1)
                    pe.wait_ge(S["hl_sb"], p + 1)
                    for i in range(TILES):
                        o = p * TOK + i * P
                        last = t.matmul(bank[6][:, i * EXPERTS:(i + 1) * EXPERTS], x_hl[:, o:o + P].bitcast(F32),
                                        par[:, ROUTW:ROUTW + EXPERTS], start=True, stop=True)
                    last.then_inc(S["logits_ready"], 1)
                    pe.wait_ge(S["gsplit_ready"], p + 1)
                    for i in range(TILES):
                        last = t.transpose(bank[7][:, bass.ts(i, P)], gsplit[:, k, i, :], ident)
                    last.then_inc(S["gT_ready"], 1)
            pe.wait_ge(S["w_split"], PIECES)
            pe.wait_ge(w2_in, 16)
            pe.wait_ge(S["sel_ready"], 1)
            pe.wait_ge(S["gT_sb"], PAIRS)
            pe.wait_ge(S["lh_sb"], PAIRS)
            pe.wait_ge(S["acc_init"], PAIRS)

            with pe.Fori(0, PAIRS) as tb:
                here = bass.ds(tb * TOK, TOK)

                def up(s):
                    pe.wait_ge(S["silu_ready"], tb * CHUNKS + max(s - 1, 0))
                    pe.wait_ge(S["h_ready"], tb * CHUNKS + max(s - 1, 0))
                    for w in range(2):
                        col = (w * CHUNKS + column(SEQ[s])) * P
                        dst = bank[2 * w + s % 2]
                        t.matmul(dst[:], w13[:, col:col + P], x_hl[:, here], start=True, stop=False)
                        t.matmul(dst[:], w13[:, col:col + P], x_lh[:, here], start=False, stop=True).then_inc(S["up_ready"], 1)

                def down(s):
                    e, m = SEQ[s]
                    half = s % 2
                    if e is None:
                        pe.wait_ge(S["tail_gated"], tb * TAILS + m + 1)
                        src, slot, first, last = htail[:, m, :], 2, m < 2, m >= TAILS - 2
                    else:
                        pe.wait_ge(S["h_ready"], tb * CHUNKS + s + 1)
                        src, slot, first, last = hbuf[:, s % 4, :], e % 2, m < 2, m >= MAIN - 2
                    if first:
                        n = next(i for i, o in enumerate(OUT_ORDER) if o[1] == (EXPERTS if e is None else e))
                        prev = 0 if e is None or e < 2 else next(i for i, o in enumerate(OUT_ORDER) if o[1] == e - 2) + 1
                        pe.wait_ge(S["out_added"], tb * OUTS + prev)
                    t.matmul(bank[4 + slot][half * C:(half + 1) * C, :], w2_sb[:, column(SEQ[s]), :], src,
                             start=first, stop=last).then_inc(S["down_done"], 1)

                for j in range(0, CHUNKS + 2, 2):
                    for s in (j, j + 1):
                        if s < CHUNKS:
                            up(s)
                            if s in GATE_AT:
                                i = GATE_AT[s]
                                pe.wait_ge(S["gb_sb"], tb * GATES + GATE_ORDER.index(i))
                                t.matmul(bank[7][:], sel_sb[:, bass.ts(i, P)], gT[:, here],
                                         start=True, stop=True).then_inc(S["gb_ready"], 1)
                    for s in (j - 2, j - 1):
                        if 0 <= s < CHUNKS:
                            down(s)
            pe.wait_ge(S["silu_ready"], PAIRS * CHUNKS)
            for p in range(PAIRS):
                pe.wait_ge(S["out_added"], (p + 1) * OUTS)
                if p >= 2:
                    pe.wait_ge(S["y_ready"], p - 1)
                t.matmul(bank[p % 2][0:C, :], par[:, FOLD:FOLD + C], acc[:, toks(p)],
                         start=True, stop=True).then_inc(S["fold_ready"], 1)


def _lay_out(i):
    f = np.float32
    x = np.ascontiguousarray(i["x"]).reshape(B, C, PX)
    packed = np.zeros((P, PACKED), f)
    for g in range(P // 2):
        packed[2 * g:2 * g + 2, PAIRAVG + 2 * g:PAIRAVG + 2 * g + 2] = 0.5
    for b in range(2):
        packed[b * C:(b + 1) * C, WRED + b * HID:WRED + (b + 1) * HID] = i["L0_conv_w_reduce"].T
        packed[b * HID:(b + 1) * HID, BRED] = i["L0_conv_b_reduce"]
    packed[2 * HID, BRED] = 1.0
    packed[:, IDENT:IDENT + P] = np.eye(P, dtype=f)
    wa, wb, wc = (i["L1_attn_att_w"][k * C:(k + 1) * C] for k in range(3))
    packed[0:C, ATTS], packed[C:P, ATTS], packed[0:C, ATTB] = wc, wa, wb
    for k, n in enumerate("zrf"):
        packed[:, GATEW + k * C:GATEW + (k + 1) * C] = i[f"L1_attn_{n}_w"].T
        packed[:, GATEB + k * C:GATEB + (k + 1) * C] = i[f"L1_attn_{n}_b"][None, :]
    packed[0:C, ROUTW:ROUTW + EXPERTS] = i["L1_ffn_router_w"].T
    packed[C:P, ROUTW:ROUTW + EXPERTS] = i["L1_ffn_router_w"].T
    packed[:, REV:REV + EXPERTS] = np.arange(EXPERTS, 0, -1)
    packed[0:C, FOLD:FOLD + C] = packed[C:P, FOLD:FOLD + C] = np.eye(C, dtype=f)
    wspan = np.zeros((2 * HID + 1, TAPS, P), f)
    ws = np.asarray(i["L0_conv_w_span"]).reshape(HID, TAPS, HID)
    bs = np.asarray(i["L0_conv_b_span"]).reshape(HID, TAPS)
    for b in range(2):
        for c in range(C):
            wspan[b * HID:(b + 1) * HID, :, b * C + c] = ws[c // 4].T
            wspan[2 * HID, :, b * C + c] = bs[c // 4]
    def chunks(w):
        main = w[:, :MAIN * P].reshape(-1, C)
        rest = w[:, MAIN * P:].reshape(-1, C)
        full = np.zeros((CHUNKS * P, C), f)
        full[:len(main)] = main
        full[len(main):len(main) + len(rest)] = rest
        return full
    w1, w3 = (np.ascontiguousarray(chunks(np.asarray(i[f"L1_ffn_w{k}"])).T) for k in (1, 3))
    w2 = chunks(np.asarray(i["L1_ffn_w2"]).transpose(0, 2, 1))
    w2 = np.ascontiguousarray(w2.reshape(CHUNKS, P, C).transpose(1, 0, 2)).reshape(P, CHUNKS * C)
    sel = np.zeros((2 * EXPERTS, GATES, P), f)
    for e in range(EXPERTS):
        for part in (e, EXPERTS + e):
            sel[part, e, :] = 1.0
            for u in range(e * REST, (e + 1) * REST):
                sel[part, EXPERTS + u // P, u % P] = 1.0
    return {"x": x, "packed": packed, "wspan": wspan.reshape(2 * HID + 1, TAPS * P), "w1": w1, "w3": w3,
            "w2": w2, "sel": sel.reshape(2 * EXPERTS, GATES * P)}


def kernel(**inputs):
    import concourse.bacc as _bacc
    from concourse.bass_utils import run_bass_kernel_spmd as _run

    arrays = _lay_out({k: np.asarray(a) for k, a in inputs.items()})
    nc = _bacc.Bacc("TRN2", target_bir_lowering=False, num_devices=1)
    args = [nc.dram_tensor(f"in_{k}", a.shape, F32, kind="ExternalInput").ap() for k, a in arrays.items()]
    out = nc.dram_tensor("out", (B, C, PX), F32, kind="ExternalOutput").ap()
    build(nc, *args, out)
    r = _run(nc, [{f"in_{k}": a for k, a in arrays.items()}], core_ids=[0])
    return r.results[0]["out"].reshape(B, C, IMG, IMG)
```

```python
from contextlib import ExitStack

import numpy as np
import concourse.bass as bass
from concourse import mybir

F32 = mybir.dt.float32
F32R = mybir.dt.float32r
ALU = mybir.AluOpType
ACT = mybir.ActivationFunctionType
AX_X = mybir.AxisListType.X

P = 128
B, C, IMG = 8, 64, 16
PX = IMG * IMG
BLOCKS = B // 2
TOK = 2 * PX
TILES = TOK // P
HID = C // 4
TAPS, PADW = 9, IMG + 2
EXPERTS, HMOE = 8, 682
MAIN = HMOE // P
REST = HMOE - MAIN * P
TAIL_EXPERTS = P // REST
TAILS = -(-EXPERTS // TAIL_EXPERTS)
CHUNKS = MAIN * EXPERTS + TAILS
PIECES = 16
PIECE = 2 * CHUNKS * P // PIECES
STAGES = 8
GATES = EXPERTS + TAILS
OUTS = EXPERTS + 1
CREDIT = 16

WIDTHS = dict(pairavg=P, wred=P, bred=1, bspan=TAPS, ident=P, atts=1, attb=1, gatew=3 * C, gateb=3 * C,
              routw=EXPERTS, fold=C)
AT_COL, PACKED = {}, 0
for _name, _width in WIDTHS.items():
    AT_COL[_name] = slice(PACKED, PACKED + _width)
    PACKED += _width
EARLY = AT_COL["atts"].start

BEFORE_TAILS = 3
SEQ = [(e, m) for e in range(BEFORE_TAILS) for m in range(MAIN)]
SEQ += [(None, q) for q in range(TAILS)]
SEQ += [(e, m) for e in range(BEFORE_TAILS, EXPERTS) for m in range(MAIN)]
POS = {c: s for s, c in enumerate(SEQ)}
TAIL = EXPERTS
OUT_ORDER = list(range(BEFORE_TAILS)) + [TAIL] + list(range(BEFORE_TAILS, EXPERTS))
LAST_OF = {e: POS[(None, TAILS - 1) if e == TAIL else (e, MAIN - 1)] for e in OUT_ORDER}


def column(chunk):
    e, m = chunk
    return (EXPERTS * MAIN + m) if e is None else e * MAIN + m


ROUTER = ("logits", "shift", "rexp", "router_a", "router_b", "router_c", "router_d", "gT")
AT_PE = {0: ["hid", "logits"], 2: ["span0"], 3: ["span1"], 4: ["span2", "span3"], 8: ["gT", "span4"], 12: ["tT"],
         16: ["n1T"], 18: ["scores0"], 19: ["scores1"], 21: ["probT0", "probT1"], 22: ["attn0"], 24: ["attn1"],
         25: ["gates0", "gates1"], 32: ["t2T"], 38: ["hl"]}
AT_ACT = {0: ["hid"], 3: ["rexp"], 7: ["gT"], 12: ["t_tok"], 16: ["k"], 19: ["exp0", "exp1"], 21: ["probT0"],
          22: ["probT1"], 23: ["attn0"], 24: ["attn1"], 25: ["tanh"], 38: ["hl"], 40: ["res"]}
AT_DVE = {0: ["hid_lo", "shift"], 1: ["tap0"], 2: ["tap1", "tap2", "tap3"], 3: ["router_a", "router_b", "tap4"],
          5: ["router_c", "router_d"], 6: ["tap5", "tap6", "tap7"], 7: ["tap8"], 8: ["res8"], 9: ["conv"],
          11: ["take0"], 12: ["st1", "mv1"], 14: ["n1a", "n1b"], 15: ["take1"], 16: ["q"], 17: ["take2", "max0"],
          19: ["max1", "norm0", "norm1"], 23: ["take3"], 24: ["bias0"], 25: ["bias1", "take4"], 27: ["mixa"],
          29: ["take5"], 30: ["mixb", "st2"], 31: ["mv2"], 34: ["n2a", "n2b"], 36: ["hi", "lo"], 38: ["take6"],
          40: ["take7"], 42: ["take8"]}
AT_POOL = {3: ["tapsum0"], 4: ["tapsum1", "tapsum2", "pow1"], 7: ["add0"], 17: ["add1", "add2"], 18: ["add3"],
           23: ["pow2"], 27: ["add4"], 28: ["add5"], 30: ["add6"], 36: ["add7"]}
BANK_OF = dict(hid=6, span0=7, span1=6, span2=7, span3=6, span4=6, tT=6, n1T=7, scores0=6, scores1=7, probT0=6,
               attn0=6, probT1=7, attn1=7, gates0=6, gates1=7, t2T=6, hl=7, logits=7, gT=7, lh=7)
FRONT_PE = ["hid", "span0", "span1", "span2", "span3", "span4", "tT", "n1T", "scores0", "scores1", "probT0",
            "attn0", "probT1", "attn1", "gates0", "gates1", "t2T", "hl", "lh"]
FRONT_ACT = ["hid", "t_tok", "k", "exp0", "exp1", "probT0", "attn0", "probT1", "attn1", "tanh", "res", "hl", "lh"]
FRONT_DVE = ["hid_lo", *(f"tap{k}" for k in range(TAPS)), "res8", "conv", "st1", "mv1", "n1a", "n1b", "q", "max0",
             "max1", "norm0", "norm1", "bias0", "bias1", "mixa", "mixb", "st2", "mv2", "n2a", "n2b", "hi", "lo"]
FRONT_POOL = ["tapsum0", "tapsum1", "tapsum2", "pow1", "pow2"]
GATE_ORDER = [0, *range(EXPERTS, GATES), *range(1, EXPERTS)]

EMPTIED = dict(hid=("hid_ready", 2, 2), tT=("t_tok_ready", 1, 1), n1T=("q_ready", 1, 1), t2T=("res_ready", 1, 1),
               hl=("hl_sb", 1, 1), lh=("x_first", 2, 2), logits=("shifted", 1, 1), gT=("gT_sb", 1, 1))
EMPTIED.update({f"span{i}": ("taps_ready", TAPS, min(2 * i + 2, TAPS)) for i in range(5)})
for _r in range(2):
    EMPTIED.update({f"scores{_r}": ("exp_ready", 4, 2 * _r + 2), f"probT{_r}": ("probT_sb", 2, _r + 1),
                    f"attn{_r}": ("cat_attn", 2, _r + 1), f"gates{_r}": ("zrf_ready", 2, _r + 1)})
USES = {name: (BANK_OF[name], *how) for name, how in EMPTIED.items()}


def parts_of(m):
    return min(TAIL_EXPERTS, EXPERTS - m * TAIL_EXPERTS)


def of_block(name):
    return name in ROUTER or name.rstrip("0123456789") in ("take", "add")


def slot_free(s):
    return s - 3 if s > 2 else s - 2


assert CHUNKS % 4 == 3
PRO_HIGHS = [4, 3, 1, 0, 3, 0, 1, 0, 2, 2, 0, 0, 0]
PRO_SPLITS = [0, 0, 3, 13, 0]
FOLD_STEPS = {5: 0, 9: 1, 13: 2}
FOLD_AT = {s + 1: p for s, p in FOLD_STEPS.items()}


def build(nc, x, packed, wspan, w1, w3, w2, out):
    with ExitStack() as ctx:
        def sb(name, shape, dt=F32, at=ctx):
            return at.enter_context(nc.sbuf_tensor(name, shape, dt))

        bank = [ctx.enter_context(nc.psum_tensor(f"bank{i}", [P, 512], F32)) for i in range(8)]

        par = sb("par", [P, PACKED])
        w13 = sb("w13", [P, 2 * CHUNKS * P], F32R)
        w2_sb = sb("w2_sb", [P, CHUNKS, C])
        span_sb = sb("span_sb", [P, TAPS * P], F32R)
        cols = {name: par[:, at] for name, at in AT_COL.items()}
        ident = cols["ident"]
        xin = sb("xin", [P, BLOCKS, PX])
        xpad = sb("xpad", [P, BLOCKS, PADW, PADW])
        x_hl = sb("x_hl", [P, BLOCKS * TOK], F32R)
        x_lh = sb("x_lh", [P, BLOCKS * TOK], F32R)
        total = sb("total", [P, BLOCKS * TOK])
        gn_st = sb("gn_st", [P, BLOCKS, 6])
        gn_mv = sb("gn_mv", [P, BLOCKS, 2])
        gn_avg = sb("gn_avg", [P, BLOCKS, 2])
        gn_d = sb("gn_d", [P, BLOCKS])
        gn_d2 = sb("gn_d2", [P, BLOCKS])
        gn_var = sb("gn_var", [P, BLOCKS])
        gn_rstd = sb("gn_rstd", [P, BLOCKS])
        gn_bias = sb("gn_bias", [P, BLOCKS])
        minus_half = sb("minus_half", [P, TILES])
        hid_raw = sb("hid_raw", [P, PX])
        hid = sb("hid", [P, PX], F32R)
        prod = sb("prod", [P, TAPS, PX])
        tapsum = sb("tapsum", [P, 2, PX])
        conv = sb("conv", [P, 3, PX])
        t_tok = sb("t_tok", [P, TILES, C])
        ln_st = sb("ln_st", [P, 2, TILES, 6])
        ln_mv = sb("ln_mv", [P, 2, TILES, 2])
        ln_ve = sb("ln_ve", [P, 2, TILES])
        ln_rs = sb("ln_rs", [P, 2, TILES])
        spare = sb("spare", [P, 1])
        n1 = sb("n1", [P, TILES, 2, C])
        qT = sb("qT", [P, TOK])
        kT = sb("kT", [P, TOK])
        cat = sb("cat", [P, TOK])
        mx = sb("mx", [P, 2, 2])
        nmx = sb("nmx", [P, 2, 2])
        ssum = sb("ssum", [P, 2, 2])
        rsum = sb("rsum", [P, 2, 2])
        prob = sb("prob", [P, 2, 2, PX])
        probT = sb("probT", [P, 2, 2, PX])
        zrf = sb("zrf", [P, TILES, 3 * C])
        gu = sb("gu", [P, TILES, C])
        gv = sb("gv", [P, TILES, C])
        t2 = sb("t2", [P, TILES, 2 * C])
        res = sb("res", [P, TOK])
        n2 = sb("n2", [P, TILES, C])
        hlh = sb("hlh", [P, TILES, 3 * C])
        hl_next = sb("hl_next", [P, TOK], F32R)
        rt = sb("rt", [P, 4, TILES, EXPERTS])
        rs = sb("rs", [P, 5, TILES])
        rprob = sb("rprob", [P, TILES, 2 * EXPERTS])
        rmax = sb("rmax", [P, TILES, 8])
        rtop = sb("rtop", [P, TILES, 8])
        rrest = sb("rrest", [P, TILES, 2 * EXPERTS])
        gT = sb("gT", [TILES * EXPERTS, P])
        gates_dram = nc.dram_tensor("gates_dram", (EXPERTS, TILES, P), F32).ap()
        raw = ExitStack()
        stage = sb("stage", [P, STAGES, PIECE], at=raw)
        span_raw = sb("span_raw", [P, TAPS * P], at=raw)
        raw.close()
        hbuf = sb("hbuf", [P, 4, TOK])
        htail = sb("htail", [P, TAILS, TOK])
        gbc = sb("gbc", [P, GATES, TOK])
        ysc = sb("ysc", [P, 2, TOK])
        ysum = sb("ysum", [P, TOK])
        y_out = sb("y_out", [C, BLOCKS, TOK])

        names = """early_in span_in late_in w2_in x_hl_in x_lh_in
        pads_zero consts_set gn_stats gn_means gn_avg_ready gn_avg_sb gn_d_ready gn_d2_ready
        gn_var_ready gn_rstd_ready gn_bias_ready xn_ready span_high span_split w_high w_split
        hidp_ready hid_ready hid_split kmap_ready taps_ready tapsum_ready conv_ready tT_ready t_tok_ready
        st_ready mv_ready ve_ready rstd_ready n1_ready n1T_ready q_ready k_ready scores_ready mx_ready nmx_ready
        exp_ready rsum_ready prob_ready probT_ready probT_sb attn_ready cat_attn gates_ready zrf_ready tanh_ready
        gu_ready gv_ready gw_ready t2_ready t2T_ready res_ready n2_ready hi_ready hi_again lo_ready hl_ready lh_ready hl_sb
        logits_ready shifted rexp_ready routed rgates_ready gT_ready gT_sb
        up_ready silu_ready h_ready tail_gated down_done gates_stored gates_zero out_taken out_added block_summed
        fold_ready y_ready stored x_first""".split()
        S = {n: ctx.enter_context(nc.semaphore(n)) for n in names}
        x_in = [ctx.enter_context(nc.semaphore(f"x_in{p}")) for p in range(BLOCKS)]
        stage_in = [ctx.enter_context(nc.semaphore(f"stage_in{i}")) for i in range(STAGES)]
        gate_in = [ctx.enter_context(nc.semaphore(f"gate_in{i}")) for i in range(GATES)]
        block = ctx.enter_context(nc.Block())

        def run_stages(stages, at, step, tb, front):
            for name in at.get(step, ()):
                if of_block(name):
                    stages(name, tb)
                elif front:
                    stages(name, tb + 1)

        @block.sync
        def _(sp):
            sp.sem_inc(S["x_hl_in"], CREDIT)
            sp.sem_inc(S["x_lh_in"], CREDIT)
            sp.sem_inc(S["gates_stored"], CREDIT)

            def load_x(p):
                sp.dma_start(xin[:, p, :], x[2 * p:2 * p + 2].rearrange("b c s -> (b c) s")).then_inc(x_in[p], 16)
            load_x(0)
            sp.dma_start(par[:, 0:EARLY], packed[:, 0:EARLY]).then_inc(S["early_in"], 16)
            for p in range(1, BLOCKS):
                load_x(p)
            sp.dma_start(span_raw[:], wspan).then_inc(S["span_in"], 16)
            sp.dma_start(par[:, EARLY:PACKED], packed[:, EARLY:PACKED]).then_inc(S["late_in"], 16)
            for i in range(PIECES):
                if i >= STAGES:
                    sp.wait_ge(S["w_split"], i - STAGES + 1)
                src = (w1, w3)[i % 2][:, bass.ts(i // 2, PIECE)]
                for h in range(2):
                    sp.dma_start(stage[h * C:(h + 1) * C, i % STAGES, :], src).then_inc(stage_in[i % STAGES], 16)
                if i == STAGES:
                    sp.dma_start(w2_sb[:], w2.rearrange("p (k c) -> p k c", c=C)).then_inc(S["w2_in"], 16)

            sp.wait_ge(S["gates_zero"], TAILS)

            def spread_gates(n):
                sp.wait_ge(S["gT_sb"], n + 1)
                sp.wait_ge(S["out_taken"], CREDIT + n * OUTS)
                sp.wait_ge(S["tail_gated"], CREDIT + n * TAILS)
                sp.dma_start(gates_dram.rearrange("e t p -> t e p"),
                             gT[:]).then_inc(S["gates_stored"], 16)
                sp.wait_ge(S["gates_stored"], CREDIT + 16 * (n + 1))
                for i in GATE_ORDER:
                    if i < EXPERTS:
                        sp.dma_start(gbc[:, i, :], gates_dram[i].rearrange("t p -> (t p)").partition_broadcast(P)).then_inc(gate_in[i], 16)
                    else:
                        first = (i - EXPERTS) * TAIL_EXPERTS
                        for k, e in enumerate(range(first, min(first + TAIL_EXPERTS, EXPERTS))):
                            sp.dma_start(gbc[k * REST:(k + 1) * REST, i, :],
                                         gates_dram[e].rearrange("t p -> (t p)").partition_broadcast(REST)).then_inc(gate_in[i], 16)

            def place_tokens(n):
                there = bass.ds(sp.snap(n * TOK), TOK)
                sp.wait_ge(S["hl_sb"], n + 1)
                sp.dma_start(x_hl[:, there].bitcast(F32), hl_next[:].bitcast(F32)).then_inc(S["x_hl_in"], 16)
                for h in range(2):
                    sp.dma_start(x_lh[h * C:(h + 1) * C, there].bitcast(F32),
                                 hl_next[(1 - h) * C:(2 - h) * C, :].bitcast(F32)).then_inc(S["x_lh_in"], 16)

            with sp.Fori(0, BLOCKS - 1) as tb:
                spread_gates(tb)
                place_tokens(tb + 1)
            spread_gates(BLOCKS - 1)
            for p in range(BLOCKS):
                sp.wait_ge(S["y_ready"], p + 1)
                sp.dma_start(out[2 * p:2 * p + 2].rearrange("b c s -> c b s"),
                             y_out[:, p, :].rearrange("c (b s) -> c b s", b=2)).then_inc(S["stored"], 16)
            sp.wait_ge(S["stored"], 16 * BLOCKS)

        @block.gpsimd
        def _(pool):
            g = nc.gpsimd
            pool.sem_inc(S["tail_gated"], CREDIT)
            pool.sem_inc(S["out_added"], CREDIT)
            g.memset(minus_half[:], -0.5).then_inc(S["consts_set"], 1)
            g.memset(xpad[:].rearrange("p a y x -> p (a y x)"), 0.0).then_inc(S["pads_zero"], 1)
            g.memset(t2[:, :, C:2 * C], 0.0).then_inc(S["consts_set"], 1)
            g.memset(rprob[:, :, EXPERTS:2 * EXPERTS], -1.0).then_inc(S["consts_set"], 1)
            g.memset(rtop[:, :, 2:8], -1.0).then_inc(S["consts_set"], 1)
            pool.wait_ge(S["consts_set"], 4)
            g.memset(kT[C:P, :], 1.0).then_inc(S["consts_set"], 1)
            pool.wait_ge(S["consts_set"], 5)
            pool.wait_ge(S["gn_var_ready"], 1)
            g.tensor_tensor(gn_rstd[:], gn_var[:], minus_half[:], ALU.pow).then_inc(S["gn_rstd_ready"], 1)
            pool.wait_ge(S["gn_rstd_ready"], 1)

            def stages(name, n):
                if name[:3] == "add":
                    i = int(name[3:])
                    pool.wait_ge(S["out_taken"], CREDIT + n * OUTS + i + 1)
                    if i:
                        pool.wait_ge(S["out_added"], CREDIT + n * (OUTS - 1) + i)
                    else:
                        pool.wait_ge(S["block_summed"], CREDIT + n)
                        pool.wait_ge(S["res_ready"], n + 1)
                    g.tensor_tensor(ysum[:], ysum[:] if i else res[:], ysc[:, i % 2, :],
                                    ALU.add).then_inc(S["out_added"], 1)
                elif name[:6] == "tapsum":
                    i = int(name[6:])
                    pool.wait_ge(S["taps_ready"], n * TAPS + 2 * (i + 2))
                    if i:
                        pool.wait_ge(S["tapsum_ready"], n * 3 + i)
                        first = tapsum[:]
                    else:
                        first = prod[:, 0:2, :]
                    g.tensor_tensor(tapsum[:], first, prod[:, 2 * i + 2:2 * i + 4, :], ALU.add).then_inc(S["tapsum_ready"], 1)
                else:
                    i = int(name[3:]) - 1
                    pool.wait_ge(S["ve_ready"], 2 * n + i + 1)
                    g.tensor_tensor(ln_rs[:, i], ln_ve[:, i], minus_half[:], ALU.pow).then_inc(S["rstd_ready"], 1)

            done = 0

            def split(count):
                nonlocal done
                for i in range(done, done + count):
                    pool.wait_ge(S["w_high"], i + 1)
                    at = bass.ts(i % 2 * (PIECES // 2) + i // 2, PIECE)
                    g.tensor_tensor(w13[C:P, at], stage[C:P, i % STAGES, :], w13[C:P, at].bitcast(F32),
                                    ALU.subtract).then_inc(S["w_split"], 1)
                done += count
            for name, count in zip(FRONT_POOL, PRO_SPLITS):
                stages(name, 0)
                if count:
                    pool.wait_ge(S["tapsum_ready"] if name[0] == "t" else S["rstd_ready"], int(name[-1]) + (name[0] == "t"))
                    split(count)
                    pool.wait_ge(S["w_split"], done)
            assert done == PIECES

            pool.wait_ge(S["w_high"], PIECES)
            pool.wait_ge(S["span_split"], 1)
            for m in range(TAILS):
                g.memset(gbc[:, EXPERTS + m, :], 0.0).then_inc(S["gates_zero"], 1)

            def experts(tb, front):
                for s in range(CHUNKS):
                    e, m = SEQ[s]
                    if e is None:
                        pool.wait_ge(S["h_ready"], CREDIT + tb * CHUNKS + s + 1)
                        pool.wait_ge(gate_in[EXPERTS + m], 16 * parts_of(m) * (tb + 1))
                        g.tensor_tensor(htail[:, m, :], hbuf[:, s % 4, :], gbc[:, EXPERTS + m, :],
                                        ALU.mult).then_inc(S["tail_gated"], 1)
                    run_stages(stages, AT_POOL, s, tb, front)

            with pool.Fori(0, BLOCKS - 1) as tb:
                experts(tb, True)
            experts(BLOCKS - 1, False)

        @block.scalar
        def _(act):
            a = nc.scalar
            act.sem_inc(S["silu_ready"], CREDIT)
            act.wait_ge(S["span_in"], 16)
            a.copy(span_sb[:], span_raw[:]).then_inc(S["span_high"], 1)

            def stages(name, n):
                if name == "hid":
                    act.wait_ge(S["hidp_ready"], n + 1)
                    a.activation(hid[:], bank[USES["hid"][0]][:, 0:PX], ACT.Relu, bias=cols["bred"]).then_inc(S["hid_ready"], 1)
                    a.activation(hid_raw[:], bank[USES["hid"][0]][:, 0:PX], ACT.Relu, bias=cols["bred"]).then_inc(S["hid_ready"], 1)
                elif name == "t_tok":
                    act.wait_ge(S["tT_ready"], n + 1)
                    a.copy(t_tok[:].rearrange("p (b h) c -> p h b c", b=2),
                           bank[USES["tT"][0]][:, 0:PX].rearrange("p (h b c) -> p h b c", h=2, b=2)).then_inc(S["t_tok_ready"], 1)
                elif name == "k":
                    act.wait_ge(S["n1T_ready"], n + 1)
                    a.copy(kT[0:C, :], bank[USES["n1T"][0]][0:C, :]).then_inc(S["k_ready"], 1)
                    a.copy(cat[0:C, :], bank[USES["n1T"][0]][0:C, :]).then_inc(S["k_ready"], 1)
                elif name[:3] == "exp":
                    r = int(name[3:])
                    act.wait_ge(S["nmx_ready"], 2 * n + r + 1)
                    for i in range(2):
                        a.activation(prob[:, r, i, :], bank[USES[f"scores{r}"][0]][:, i * PX:(i + 1) * PX], ACT.Exp,
                                     bias=nmx[:, r, i:i + 1], accum_out=ssum[:, r, i:i + 1]).then_inc(S["exp_ready"], 1)
                elif name[:5] == "probT":
                    r = int(name[5:])
                    act.wait_ge(S["probT_ready"], 2 * n + r + 1)
                    a.copy(probT[:, r].rearrange("p j i -> p (j i)"), bank[USES[name][0]][:]).then_inc(S["probT_sb"], 1)
                elif name[:4] == "attn":
                    r = int(name[4:])
                    act.wait_ge(S["attn_ready"], 2 * n + r + 1)
                    a.copy(cat[C:P, r * PX:(r + 1) * PX], bank[USES[name][0]][C:P, 0:PX]).then_inc(S["cat_attn"], 1)
                elif name == "tanh":
                    act.wait_ge(S["zrf_ready"], 2 * n + 2)
                    a.activation(zrf[:, :, 0:C], zrf[:, :, 0:C], ACT.Tanh).then_inc(S["tanh_ready"], 1)
                    a.activation(zrf[:, :, C:3 * C], zrf[:, :, C:3 * C], ACT.Tanh, scale=0.5).then_inc(S["tanh_ready"], 1)
                elif name == "res":
                    act.wait_ge(S["t2T_ready"], n + 1)
                    a.copy(res[:], bank[USES["t2T"][0]][:]).then_inc(S["res_ready"], 1)
                elif name in ("hl", "lh"):
                    act.wait_ge(S[f"{name}_ready"], n + 1)
                    source = bank[USES[name][0]]
                    if isinstance(n, int):
                        a.copy((x_hl if name == "hl" else x_lh)[:, 0:TOK], source[:]).then_inc(S["x_first"], 1)
                    else:
                        act.wait_ge(S["x_hl_in"], CREDIT + 16 * (n - 1))
                        act.wait_ge(S["x_lh_in"], CREDIT + 32 * (n - 1))
                        act.wait_ge(S["logits_ready"], n)
                    if name == "hl":
                        a.copy(hl_next[:], source[:]).then_inc(S["hl_sb"], 1)
                elif name == "rexp":
                    act.wait_ge(S["shifted"], n + 1)
                    a.activation(rt[:, 1], rt[:, 0], ACT.Exp).then_inc(S["rexp_ready"], 1)
                elif name == "gT":
                    act.wait_ge(S["gT_ready"], n + 1)
                    act.wait_ge(S["gates_stored"], CREDIT + 16 * n)
                    a.copy(gT[:], bank[USES["gT"][0]][0:TILES * EXPERTS, 0:P]).then_inc(S["gT_sb"], 1)
                else:
                    raise KeyError(name)

            done = 0

            def high(count):
                nonlocal done
                for i in range(done, done + count):
                    act.wait_ge(stage_in[i % STAGES], 32 * (i // STAGES + 1))
                    at = bass.ts(i % 2 * (PIECES // 2) + i // 2, PIECE)
                    a.copy(w13[:, at], stage[:, i % STAGES, :]).then_inc(S["w_high"], 1)
                done += count
            for name, count in zip(FRONT_ACT, PRO_HIGHS):
                stages(name, 0)
                high(count)
            assert done == PIECES

            def experts(tb, front):
                for s in range(CHUNKS):
                    act.wait_ge(S["up_ready"], tb * 2 * CHUNKS + 2 * s + 1)
                    act.wait_ge(S["down_done"], CREDIT + tb * CHUNKS + slot_free(s))
                    a.activation(hbuf[:, s % 4, :], bank[s % 2][:], ACT.Silu).then_inc(S["silu_ready"], 1)
                    run_stages(stages, AT_ACT, s, tb, front)
                    if not front and s in FOLD_AT:
                        copy_out(FOLD_AT[s])

            def copy_out(p):
                act.wait_ge(S["fold_ready"], p + 1)
                a.copy(y_out[:, p, :], bank[6][0:C, :]).then_inc(S["y_ready"], 1)

            with act.Fori(0, BLOCKS - 1) as tb:
                experts(tb, True)
            experts(BLOCKS - 1, False)
            copy_out(BLOCKS - 1)

        @block.vector
        def _(dve):
            v = nc.vector
            dve.sem_inc(S["h_ready"], CREDIT)
            dve.sem_inc(S["out_taken"], CREDIT)
            dve.sem_inc(S["block_summed"], CREDIT)
            for p in range(BLOCKS):
                dve.wait_ge(x_in[p], 16)
                v.bn_stats(gn_st[:, p], xin[:, p, :]).then_inc(S["gn_stats"], 1)
            for p in range(BLOCKS):
                dve.wait_ge(S["gn_stats"], p + 1)
                v.bn_aggr(gn_mv[:, p], gn_st[:, p]).then_inc(S["gn_means"], 1)
            dve.wait_ge(S["gn_avg_ready"], 1)
            v.tensor_copy(gn_avg[:].rearrange("p a b -> p (a b)"), bank[0][:, 0:2 * BLOCKS]).then_inc(S["gn_avg_sb"], 1)
            dve.wait_ge(S["gn_avg_sb"], 1)
            v.tensor_tensor(gn_d[:], gn_mv[:, :, 0], gn_avg[:, :, 0], ALU.subtract).then_inc(S["gn_d_ready"], 1)
            dve.wait_ge(S["gn_d_ready"], 1)
            v.tensor_tensor(gn_d2[:], gn_d[:], gn_d[:], ALU.mult).then_inc(S["gn_d2_ready"], 1)
            dve.wait_ge(S["gn_d2_ready"], 1)
            v.scalar_tensor_tensor(gn_var[:], gn_d2[:], 1e-5, gn_avg[:, :, 1], ALU.add, ALU.add).then_inc(S["gn_var_ready"], 1)
            dve.wait_ge(S["span_high"], 1)
            v.tensor_tensor(span_sb[C:P, :], span_raw[C:P, :], span_sb[C:P, :].bitcast(F32), ALU.subtract).then_inc(S["span_split"], 1)
            dve.wait_ge(S["gn_rstd_ready"], 1)
            v.scalar_tensor_tensor(gn_bias[:], gn_avg[:, :, 0], -1.0, gn_rstd[:], ALU.mult, ALU.mult).then_inc(S["gn_bias_ready"], 1)
            dve.wait_ge(S["gn_bias_ready"], 1)
            dve.wait_ge(S["pads_zero"], 1)
            for p in range(BLOCKS):
                v.tensor_scalar(xpad[:, p, 1:1 + IMG, 1:1 + IMG], xin[:, p, :].rearrange("p (y x) -> p y x", y=IMG),
                                gn_rstd[:, p:p + 1], gn_bias[:, p:p + 1], ALU.mult, ALU.add).then_inc(S["xn_ready"], 1)
            dve.wait_ge(S["xn_ready"], BLOCKS)

            LINKS = 8
            link_at = [0]

            def link(n, ins):
                link_at[0] += 1
                ins.then_inc(S["routed"], 1)
                dve.wait_ge(S["routed"], n * LINKS + link_at[0])

            def wide(i):
                return rs[:, i].rearrange("p (t e) -> p t e", e=1).to_broadcast([P, TILES, EXPERTS])

            def stages(name, n):
                if name[:4] == "take":
                    i = int(name[4:])
                    e = OUT_ORDER[i]
                    dve.wait_ge(S["down_done"], CREDIT + n * CHUNKS + LAST_OF[e] + 1)
                    dve.wait_ge(S["out_added"], CREDIT + n * (OUTS - 1) + max(i - 1, 0))
                    if e == TAIL:
                        v.tensor_copy(ysc[:, i % 2, :], bank[4 + i % 2][:]).then_inc(S["out_taken"], 1)
                    else:
                        dve.wait_ge(gate_in[e], 16 * (n + 1))
                        v.tensor_tensor(ysc[:, i % 2, :], bank[4 + i % 2][:], gbc[:, e, :],
                                        ALU.mult).then_inc(S["out_taken"], 1)
                elif name == "hid_lo":
                    dve.wait_ge(S["hid_ready"], 2 * n + 2)
                    for r in (32, 96):
                        v.tensor_tensor(hid[r:r + 32, :], hid_raw[r:r + 32, :], hid[r:r + 32, :].bitcast(F32),
                                        ALU.subtract).then_inc(S["hid_split"], 1)
                elif name[:3] == "tap":
                    k = int(name[3:])
                    dve.wait_ge(S["kmap_ready"], 5 * n + k // 2 + 1)
                    window = xpad[:, n, k // 3:k // 3 + IMG, k % 3:k % 3 + IMG] if isinstance(n, int) else \
                        xpad[:, bass.ds(n, 1), k // 3:k // 3 + IMG, k % 3:k % 3 + IMG].rearrange("p a y x -> p (a y) x")
                    kmap = bank[USES[f"span{k // 2}"][0]][:, k % 2 * PX:(k % 2 + 1) * PX]
                    v.scalar_tensor_tensor(prod[:, k, :].rearrange("p (y x) -> p y x", y=IMG),
                                           kmap.rearrange("p (y x) -> p y x", y=IMG),
                                           cols["bspan"][:, k:k + 1], window, ALU.add, ALU.mult).then_inc(S["taps_ready"], 1)
                elif name == "res8":
                    source = xin[:, n, :] if isinstance(n, int) else xin[:, bass.ds(n, 1), :].rearrange("p a s -> p (a s)")
                    dve.wait_ge(S["taps_ready"], (n + 1) * TAPS)
                    v.tensor_tensor(conv[:, 0, :], prod[:, TAPS - 1, :], source, ALU.add).then_inc(S["conv_ready"], 1)
                elif name == "conv":
                    dve.wait_ge(S["tapsum_ready"], 3 * n + 3)
                    v.tensor_tensor(conv[:, 1, :], tapsum[:, 0, :], tapsum[:, 1, :], ALU.add).then_inc(S["conv_ready"], 1)
                    dve.wait_ge(S["conv_ready"], 3 * n + 2)
                    v.tensor_tensor(conv[:, 2, :], conv[:, 0, :], conv[:, 1, :], ALU.add).then_inc(S["conv_ready"], 1)
                elif name[:2] in ("st", "mv"):
                    i = int(name[2:]) - 1
                    src, ready = ((t_tok, "t_tok_ready"), (t2, "t2_ready"))[i]
                    if name[:2] == "st":
                        dve.wait_ge(S[ready], n + 1)
                        for t in range(TILES):
                            v.bn_stats(ln_st[:, i, t], src[:, t, 0:C]).then_inc(S["st_ready"], 1)
                        return
                    dve.wait_ge(S["st_ready"], (2 * n + i + 1) * TILES)
                    v.memset(spare[:], 0.0)
                    for t in range(TILES):
                        v.bn_aggr(ln_mv[:, i, t], ln_st[:, i, t]).then_inc(S["mv_ready"], 1)
                    dve.wait_ge(S["mv_ready"], (2 * n + i + 1) * TILES)
                    v.tensor_scalar_add(ln_ve[:, i], ln_mv[:, i, :, 1], 1e-5).then_inc(S["ve_ready"], 1)
                elif name in ("n1a", "n1b"):
                    half = "ab".index(name[-1]) * 2
                    dve.wait_ge(S["rstd_ready"], 2 * n + 1)
                    for t in (half, half + 1):
                        v.tensor_scalar(n1[:, t], t_tok[:, t:t + 1, :].to_broadcast([P, 2, C]), ln_mv[:, 0, t, 0:1],
                                        ln_rs[:, 0, t:t + 1], ALU.subtract, ALU.mult).then_inc(S["n1_ready"], 1)
                elif name == "q":
                    dve.wait_ge(S["k_ready"], 2 * n + 2)
                    v.tensor_scalar(qT[:], bank[USES["n1T"][0]][:], cols["atts"], cols["attb"], ALU.mult, ALU.add).then_inc(S["q_ready"], 1)
                elif name[:3] == "max":
                    r = int(name[3:])
                    dve.wait_ge(S["scores_ready"], 2 * n + r + 1)
                    v.tensor_reduce(mx[:, r], bank[USES[name.replace("max", "scores")][0]][:].rearrange("p (i j) -> p i j", i=2), AX_X, ALU.max).then_inc(S["mx_ready"], 1)
                    dve.wait_ge(S["mx_ready"], 2 * n + r + 1)
                    v.tensor_scalar_mul(nmx[:, r], mx[:, r], -1.0).then_inc(S["nmx_ready"], 1)
                elif name[:4] == "norm":
                    r = int(name[4:])
                    dve.wait_ge(S["exp_ready"], 4 * n + 2 * r + 2)
                    v.reciprocal(rsum[:, r], ssum[:, r]).then_inc(S["rsum_ready"], 1)
                    dve.wait_ge(S["rsum_ready"], 2 * n + r + 1)
                    for i in range(2):
                        v.tensor_scalar_mul(prob[:, r, i, :], prob[:, r, i, :], rsum[:, r, i:i + 1]).then_inc(S["prob_ready"], 1)
                elif name[:4] == "bias":
                    h = int(name[4:])
                    dve.wait_ge(S["gates_ready"], 2 * n + h + 1)
                    v.tensor_tensor(zrf[:, 2 * h:2 * h + 2, :], bank[USES[f"gates{h}"][0]][:, 0:6 * C].rearrange("p (t c) -> p t c", t=2),
                                    cols["gateb"].rearrange("p (t c) -> p t c", t=1).to_broadcast([P, 2, 3 * C]),
                                    ALU.add).then_inc(S["zrf_ready"], 1)
                elif name == "mixa":
                    dve.wait_ge(S["tanh_ready"], 2 * n + 2)
                    v.scalar_tensor_tensor(gu[:], zrf[:, :, C:2 * C], 1.0, n1[:, :, 0, :], ALU.add, ALU.mult).then_inc(S["gu_ready"], 1)
                    v.scalar_tensor_tensor(gv[:], zrf[:, :, 2 * C:3 * C], 1.0, zrf[:, :, 0:C], ALU.add, ALU.mult).then_inc(S["gv_ready"], 1)
                elif name == "mixb":
                    dve.wait_ge(S["gu_ready"], n + 1)
                    dve.wait_ge(S["gv_ready"], n + 1)
                    v.tensor_tensor(gu[:], gu[:], gv[:], ALU.add).then_inc(S["gw_ready"], 1)
                    dve.wait_ge(S["gw_ready"], n + 1)
                    v.scalar_tensor_tensor(t2[:, :, 0:C], gu[:], 0.5, t_tok[:], ALU.mult, ALU.add).then_inc(S["t2_ready"], 1)
                elif name in ("n2a", "n2b"):
                    half = "ab".index(name[-1]) * 2
                    dve.wait_ge(S["rstd_ready"], 2 * n + 2)
                    for t in (half, half + 1):
                        v.tensor_scalar(n2[:, t, :], t2[:, t, 0:C], ln_mv[:, 1, t, 0:1],
                                        ln_rs[:, 1, t:t + 1], ALU.subtract, ALU.mult).then_inc(S["n2_ready"], 1)
                elif name == "hi":
                    dve.wait_ge(S["n2_ready"], (n + 1) * TILES)
                    high = hlh[:].bitcast(F32R)
                    v.tensor_copy(high[:, :, 0:C], n2[:]).then_inc(S["hi_ready"], 1)
                    if isinstance(n, int):
                        v.tensor_copy(high[:, :, 2 * C:3 * C], n2[:]).then_inc(S["hi_again"], 1)
                elif name == "lo":
                    dve.wait_ge(S["hi_ready"], n + 1)
                    v.tensor_tensor(hlh[:, :, C:2 * C], n2[:], hlh[:, :, 0:C], ALU.subtract).then_inc(S["lo_ready"], 1)
                elif name == "shift":
                    link_at[0] = 0
                    dve.wait_ge(S["logits_ready"], n + 1)
                    logits = bank[USES["logits"][0]][:, 0:TILES * EXPERTS].rearrange("p (t e) -> p t e", e=EXPERTS)
                    link(n, v.tensor_reduce(rs[:, 0], logits, AX_X, ALU.max))
                    v.tensor_tensor(rt[:, 0], logits, wide(0), ALU.subtract).then_inc(S["shifted"], 1)
                elif name == "router_a":
                    dve.wait_ge(S["rexp_ready"], n + 1)
                    link(n, v.tensor_reduce(rs[:, 1], rt[:, 1], AX_X, ALU.add))
                    link(n, v.reciprocal(rs[:, 2], rs[:, 1]))
                    link(n, v.tensor_tensor(rprob[:, :, 0:EXPERTS], rt[:, 1], wide(2), ALU.mult))
                elif name == "router_b":
                    v.memset(spare[:], 0.0)
                    for t in range(TILES):
                        last = v.max(rmax[:, t, :], rprob[:, t, 0:EXPERTS])
                    link(n, last)
                    v.tensor_copy(rtop[:, :, 0:2], rmax[:, :, 0:2])
                    link(n, v.scalar_tensor_tensor(rs[:, 3], rmax[:, :, 0], 1e-9, rmax[:, :, 1], ALU.add, ALU.add))
                elif name == "router_c":
                    v.memset(spare[:], 0.0)
                    for t in range(TILES):
                        v.match_replace(rrest[:, t, :], rtop[:, t, :], rprob[:, t, :], 0.0)
                    link(n, v.reciprocal(rs[:, 4], rs[:, 3]))
                elif name == "router_d":
                    link(n, v.tensor_tensor(rt[:, 2], rprob[:, :, 0:EXPERTS], rrest[:, :, 0:EXPERTS], ALU.subtract))
                    assert link_at[0] == LINKS
                    v.tensor_tensor(rt[:, 3], rt[:, 2], wide(4), ALU.mult).then_inc(S["rgates_ready"], 1)
                else:
                    raise KeyError(name)

            for name in FRONT_DVE:
                stages(name, 0)
            dve.wait_ge(S["consts_set"], 5)

            def experts(tb, front):
                here = bass.ds(tb * TOK, TOK)

                for s in range(CHUNKS):
                    dve.wait_ge(S["silu_ready"], CREDIT + tb * CHUNKS + s + 1)
                    dve.wait_ge(S["up_ready"], tb * 2 * CHUNKS + 2 * s + 2)
                    v.tensor_tensor(hbuf[:, s % 4, :], hbuf[:, s % 4, :], bank[2 + s % 2][:], ALU.mult).then_inc(S["h_ready"], 1)
                    run_stages(stages, AT_DVE, s, tb, front)
                dve.wait_ge(S["out_taken"], CREDIT + (tb + 1) * OUTS)
                dve.wait_ge(S["out_added"], CREDIT + (tb + 1) * (OUTS - 1))
                v.tensor_tensor(total[:, here], ysum[:], ysc[:, (OUTS - 1) % 2, :], ALU.add).then_inc(S["block_summed"], 1)

            with dve.Fori(0, BLOCKS - 1) as tb:
                experts(tb, True)
            experts(BLOCKS - 1, False)

        @block.tensor
        def _(pe):
            t = nc.tensor
            pe.sem_inc(S["down_done"], CREDIT)
            pe.wait_ge(S["early_in"], 16)
            pe.wait_ge(S["gn_means"], BLOCKS)
            t.matmul(bank[0][:, 0:2 * BLOCKS], cols["pairavg"], gn_mv[:].rearrange("p a b -> p (a b)"),
                     start=True, stop=True).then_inc(S["gn_avg_ready"], 1)

            def emptied(name, n):
                _, sem, per, at = USES[name]
                pe.wait_ge(S[sem], n * per + at)

            def stages(name, n):
                into = bank[USES[name][0]]
                if name == "hid":
                    pe.wait_ge(S["xn_ready"], BLOCKS)
                    window = xpad[:, n, 1:1 + IMG, 1:1 + IMG] if isinstance(n, int) else \
                        xpad[:, bass.ds(n, 1), 1:1 + IMG, 1:1 + IMG]
                    t.matmul(into[:, 0:PX], cols["wred"], window, start=True, stop=True).then_inc(S["hidp_ready"], 1)
                elif name[:4] == "span":
                    i = int(name[4:])
                    if i == 0:
                        pe.wait_ge(S["hid_split"], 2 * n + 2)
                    for k in range(2 * i, min(2 * i + 2, TAPS)):
                        last = t.matmul(into[:, k % 2 * PX:(k % 2 + 1) * PX], span_sb[:, bass.ts(k, P)], hid[:],
                                        start=True, stop=True)
                    last.then_inc(S["kmap_ready"], 1)
                elif name == "tT":
                    pe.wait_ge(S["conv_ready"], 3 * n + 3)
                    for i in range(2):
                        last = t.transpose(into[:, bass.ts(i, P)], conv[:, 2, bass.ts(i, P)], ident)
                    last.then_inc(S["tT_ready"], 1)
                elif name == "n1T":
                    pe.wait_ge(S["n1_ready"], (n + 1) * TILES)
                    for i in range(TILES):
                        last = t.transpose(into[:, bass.ts(i, P)], n1[:, i].rearrange("p a c -> p (a c)"), ident)
                    last.then_inc(S["n1T_ready"], 1)
                elif name[:6] == "scores":
                    r = int(name[6:])
                    pe.wait_ge(S["q_ready"], n + 1)
                    pe.wait_ge(S["k_ready"], 2 * n + 1)
                    for i in range(2):
                        q = r * PX + i * P
                        last = t.matmul(into[:, i * PX:(i + 1) * PX], qT[:, q:q + P], kT[:, r * PX:(r + 1) * PX],
                                        start=True, stop=True)
                    last.then_inc(S["scores_ready"], 1)
                elif name[:5] == "probT":
                    r = int(name[5:])
                    pe.wait_ge(S["prob_ready"], 4 * n + 2 * r + 2)
                    for j in range(2):
                        for i in range(2):
                            o = j * PX + i * P
                            last = t.transpose(into[:, o:o + P], prob[:, r, i, bass.ts(j, P)], ident)
                    last.then_inc(S["probT_ready"], 1)
                elif name[:4] == "attn":
                    r = int(name[4:])
                    pe.wait_ge(S["probT_sb"], 2 * n + r + 1)
                    for j in range(2):
                        last = t.matmul(into[C:P, 0:PX], n1[:, 2 * r + j, 0, :], probT[:, r, j, :],
                                        start=j == 0, stop=j == 1)
                    last.then_inc(S["attn_ready"], 1)
                elif name[:5] == "gates":
                    h = int(name[5:])
                    pe.wait_ge(S["cat_attn"], 2 * n + 2)
                    pe.wait_ge(S["k_ready"], 2 * n + 2)
                    for i in range(2):
                        k = (2 * h + i) * P
                        last = t.matmul(into[:, i * 3 * C:(i + 1) * 3 * C], cat[:, k:k + P], cols["gatew"],
                                        start=True, stop=True)
                    last.then_inc(S["gates_ready"], 1)
                elif name == "t2T":
                    pe.wait_ge(S["t2_ready"], n + 1)
                    for i in range(TILES):
                        last = t.transpose(into[:, bass.ts(i, P)], t2[:, i, :], ident)
                    last.then_inc(S["t2T_ready"], 1)
                elif name in ("hl", "lh"):
                    pe.wait_ge(S["lo_ready"], n + 1)
                    if isinstance(n, int):
                        pe.wait_ge(S["hi_again"], n + 1)
                    o = 0 if name == "hl" else C
                    for i in range(TILES):
                        last = t.transpose(into[:, bass.ts(i, P)], hlh[:, i, o:o + P], ident)
                    last.then_inc(S[f"{name}_ready"], 1)
                elif name == "logits":
                    pe.wait_ge(S["hl_sb"], n + 1)
                    for i in range(TILES):
                        last = t.matmul(into[:, i * EXPERTS:(i + 1) * EXPERTS], hl_next[:, bass.ts(i, P)].bitcast(F32),
                                        cols["routw"], start=True, stop=True)
                    last.then_inc(S["logits_ready"], 1)
                elif name == "gT":
                    pe.wait_ge(S["rgates_ready"], n + 1)
                    t.transpose(into[0:TILES * EXPERTS, 0:P], rt[:, 3].rearrange("p t e -> p (t e)"),
                                ident).then_inc(S["gT_ready"], 1)
                else:
                    raise KeyError(name)

            before = {}
            for name in FRONT_PE:
                if name == "span0":
                    pe.wait_ge(S["span_split"], 1)
                if name == "n1T":
                    pe.wait_ge(S["late_in"], 16)
                    pe.wait_ge(S["consts_set"], 5)
                if USES[name][0] in before:
                    emptied(before[USES[name][0]], 0)
                before[USES[name][0]] = name
                stages(name, 0)
            pe.wait_ge(S["x_first"], 2)
            pe.wait_ge(S["w2_in"], 16)
            pe.wait_ge(S["w_split"], PIECES)

            def experts(tb, front):
                here = bass.ds(tb * TOK, TOK)
                before = {}
                for names in AT_PE.values():
                    for name in names:
                        before[USES[name][0]] = (name, tb - 1 if of_block(name) else tb)

                def up(s):
                    used = tb * CHUNKS + (s - 1 if s else 0)
                    for w in range(2):
                        pe.wait_ge(S[("silu_ready", "h_ready")[w]], CREDIT + used)
                        col = (w * CHUNKS + column(SEQ[s])) * P
                        dst = bank[2 * w + s % 2]
                        t.matmul(dst[:], w13[:, col:col + P], x_hl[:, here], start=True, stop=False)
                        t.matmul(dst[:], w13[:, col:col + P], x_lh[:, here], start=False, stop=True).then_inc(S["up_ready"], 1)

                def down(s):
                    e, m = SEQ[s]
                    i = OUT_ORDER.index(TAIL if e is None else e)
                    if e is None:
                        pe.wait_ge(S["tail_gated"], CREDIT + tb * TAILS + m + 1)
                        src, ends = htail[:, m, :], TAILS - 2
                    else:
                        pe.wait_ge(S["h_ready"], CREDIT + tb * CHUNKS + s + 1)
                        src, ends = hbuf[:, s % 4, :], MAIN - 2
                    if m < 2:
                        pe.wait_ge(S["out_taken"], CREDIT + tb * OUTS + max(i - 1, 0))
                    half = s % 2
                    t.matmul(bank[4 + i % 2][half * C:(half + 1) * C, :], w2_sb[:, column(SEQ[s]), :], src,
                             start=m < 2, stop=m >= ends).then_inc(S["down_done"], 1)

                pe.wait_ge(S["x_hl_in"], CREDIT + 16 * tb)
                pe.wait_ge(S["x_lh_in"], CREDIT + 32 * tb)
                for j in range(0, CHUNKS + 2, 2):
                    for s in (j, j + 1):
                        if s >= CHUNKS:
                            continue
                        up(s)
                        for name in AT_PE.get(s, ()):
                            own = of_block(name)
                            if own or front:
                                n = tb if own else tb + 1
                                emptied(*before[USES[name][0]])
                                before[USES[name][0]] = (name, n)
                                stages(name, n)
                        if not front and s in FOLD_STEPS:
                            fold(FOLD_STEPS[s])
                    for s in (j - 2, j - 1):
                        if 0 <= s < CHUNKS:
                            down(s)

            def fold(p):
                pe.wait_ge(S["block_summed"], CREDIT + p + 1)
                if p:
                    pe.wait_ge(S["y_ready"], p)
                t.matmul(bank[6][0:C, :], cols["fold"], total[:, p * TOK:(p + 1) * TOK],
                         start=True, stop=True).then_inc(S["fold_ready"], 1)

            with pe.Fori(0, BLOCKS - 1) as tb:
                experts(tb, True)
            experts(BLOCKS - 1, False)
            fold(BLOCKS - 1)


def _lay_out(i):
    f = np.float32
    x = np.ascontiguousarray(i["x"]).reshape(B, C, PX)
    packed = np.zeros((P, PACKED), f)

    def put(name):
        return packed[:, AT_COL[name]]
    for g in range(P // 2):
        put("pairavg")[2 * g:2 * g + 2, 2 * g:2 * g + 2] = 0.5
    bs = np.asarray(i["L0_conv_b_span"]).reshape(HID, TAPS)
    for r in range(4):
        for b in range(2):
            o = (2 * r + b) * HID
            put("wred")[b * C:(b + 1) * C, o:o + HID] = i["L0_conv_w_reduce"].T
            put("bred")[o:o + HID, 0] = i["L0_conv_b_reduce"]
    for c in range(P):
        put("bspan")[c] = bs[c % C // 4]
    put("ident")[:] = np.eye(P, dtype=f)
    wa, wb, wc = (i["L1_attn_att_w"][k * C:(k + 1) * C] for k in range(3))
    put("atts")[0:C, 0], put("atts")[C:P, 0], put("attb")[0:C, 0] = wc, wa, wb
    for k, n in enumerate("zrf"):
        put("gatew")[:, k * C:(k + 1) * C] = i[f"L1_attn_{n}_w"].T
        put("gateb")[:, k * C:(k + 1) * C] = i[f"L1_attn_{n}_b"][None, :]
    put("routw")[0:C] = put("routw")[C:P] = i["L1_ffn_router_w"].T
    put("fold")[0:C] = put("fold")[C:P] = np.eye(C, dtype=f)
    wspan = np.zeros((P, TAPS, P), f)
    ws = np.asarray(i["L0_conv_w_span"]).reshape(HID, TAPS, HID)
    for r in range(4):
        for b in range(2):
            o = (2 * r + b) * HID
            for c in range(C):
                wspan[o:o + HID, :, b * C + c] = ws[c // 4].T
    def chunks(w):
        full = np.zeros((CHUNKS * P, C), f)
        full[:EXPERTS * MAIN * P] = w[:, :MAIN * P].reshape(-1, C)
        for e in range(EXPERTS):
            o = (EXPERTS * MAIN + e // TAIL_EXPERTS) * P + e % TAIL_EXPERTS * REST
            full[o:o + REST] = w[e, MAIN * P:]
        return full
    w1, w3 = (np.ascontiguousarray(chunks(np.asarray(i[f"L1_ffn_w{k}"])).T) for k in (1, 3))
    w2 = chunks(np.asarray(i["L1_ffn_w2"]).transpose(0, 2, 1))
    w2 = np.ascontiguousarray(w2.reshape(CHUNKS, P, C).transpose(1, 0, 2)).reshape(P, CHUNKS * C)
    return {"x": x, "packed": packed, "wspan": wspan.reshape(P, TAPS * P), "w1": w1, "w3": w3,
            "w2": w2}


def kernel(**inputs):
    import concourse.bacc as _bacc
    from concourse.bass_utils import run_bass_kernel_spmd as _run

    arrays = _lay_out({k: np.asarray(a) for k, a in inputs.items()})
    nc = _bacc.Bacc("TRN2", target_bir_lowering=False, num_devices=1)
    args = [nc.dram_tensor(f"in_{k}", a.shape, F32, kind="ExternalInput").ap() for k, a in arrays.items()]
    out = nc.dram_tensor("out", (B, C, PX), F32, kind="ExternalOutput").ap()
    build(nc, *args, out)
    r = _run(nc, [{f"in_{k}": a for k, a in arrays.items()}], core_ids=[0])
    return r.results[0]["out"].reshape(B, C, IMG, IMG)
```

```python
from contextlib import ExitStack

import numpy as np
import concourse.bass as bass
from concourse import mybir

F32 = mybir.dt.float32
F32R = mybir.dt.float32r
BF16 = mybir.dt.bfloat16
ALU = mybir.AluOpType
ACT = mybir.ActivationFunctionType
AX_X = mybir.AxisListType.X

P = 128
B, C, IMG = 8, 64, 16
PX = IMG * IMG
BLOCKS = B // 2
TOK = 2 * PX
TILES = TOK // P
HID = C // 4
TAPS, PADW = 9, IMG + 2
EXPERTS, HMOE = 8, 682
MAIN = HMOE // P
REST = HMOE - MAIN * P
TAIL_EXPERTS = P // REST
TAILS = -(-EXPERTS // TAIL_EXPERTS)
CHUNKS = MAIN * EXPERTS + TAILS
PIECES = 16
PIECE = 2 * CHUNKS * P // PIECES
GATES = EXPERTS + TAILS
OUTS = EXPERTS + 1
CREDIT = 64

WIDTHS = dict(pairavg=P, wred=P, bred=1, bspan=TAPS, ident=P, atts=1, attb=1, gatew=3 * C, gateb=3 * C,
              fold=C)
AT_COL, PACKED = {}, 0
for _name, _width in WIDTHS.items():
    AT_COL[_name] = slice(PACKED, PACKED + _width)
    PACKED += _width
EARLY = AT_COL["atts"].start

ROUTER_CHUNK, ROUTER_ROWS = TAILS - 1, 32
MAINS = [(e, m) for e in range(EXPERTS) for m in range(MAIN)]
SEQ = [(None, ROUTER_CHUNK)] + [(None, q) for q in range(TAILS) if q != ROUTER_CHUNK] + MAINS
POS = {c: s for s, c in enumerate(SEQ)}
BEFORE_TAILS = 3
DOWNS = MAINS[:BEFORE_TAILS * MAIN] + [(None, q) for q in range(TAILS)] + MAINS[BEFORE_TAILS * MAIN:]
DOWN = {c: d for d, c in enumerate(DOWNS)}
TAIL = EXPERTS
OUT_ORDER = list(range(BEFORE_TAILS)) + [TAIL] + list(range(BEFORE_TAILS, EXPERTS))
LAST_OF = {e: DOWN[(None, TAILS - 1) if e == TAIL else (e, MAIN - 1)] for e in OUT_ORDER}
SLOTS = 5
assert len(MAINS) % SLOTS == 0


def downs_at(j):
    first = BEFORE_TAILS * MAIN - 1
    assert first % 2 == 0
    at = first + 2 * TAILS
    if j < at:
        return range(max(j - 2 * TAILS, 0), max(j - 2 * TAILS + 2, 0))
    if j < at + 4:
        return range(first + 2 * (j - at), first + 2 * (j - at) + 4)
    return range(j - 2, min(j, CHUNKS))


assert [d for j in range(0, CHUNKS + 2, 2) for d in downs_at(j)] == list(range(CHUNKS))


def freed_by(s):
    e, m = SEQ[s]
    if e is None:
        return DOWN[(None, m)] + 1 - CHUNKS
    u = s - TAILS
    return DOWN[MAINS[u - SLOTS]] + 1 - (CHUNKS if u < SLOTS else 0)


def rest_row(e):
    return e % TAIL_EXPERTS * REST + (ROUTER_ROWS if e // TAIL_EXPERTS == ROUTER_CHUNK else 0)


def column(chunk):
    e, m = chunk
    return (EXPERTS * MAIN + m) if e is None else e * MAIN + m


ROUTER = ("logits", "shift", "rexp", "router_a", "router_b", "router_c", "router_d", "gT")
AT_PE = {0: ["hid"], 2: ["span0"], 3: ["span1"], 5: ["logits"], 7: ["span2"], 9: ["span3"], 11: ["gT"], 12: ["span4"],
         14: ["tT"], 18: ["n1T"], 20: ["scores0"], 21: ["scores1"], 23: ["probT0", "probT1"], 24: ["attn0", "attn1"],
         26: ["gates0"], 27: ["gates1"], 40: ["hl"], 42: ["t2T"]}
AT_ACT = {0: ["hid"], 7: ["rexp"], 10: ["gT"], 14: ["t_tok"], 18: ["k"], 21: ["exp0", "exp1"],
          22: ["probT0", "probT1"], 23: ["attn0"], 24: ["attn1"], 27: ["tanh"], 39: ["hl"], 42: ["res"]}
AT_DVE = {0: ["hid_lo"], 2: ["tap0", "tap1"], 3: ["tap2"], 5: ["shift", "tap3"], 6: ["tap4"],
          7: ["tap5", "router_a", "router_b", "router_c"], 9: ["router_d", "tap6"], 10: ["tap7"], 11: ["tap8"],
          12: ["res8", "conv"], 14: ["st1"], 15: ["mv1", "take0"], 16: ["n1a", "n1b"], 18: ["q", "take1"],
          19: ["max0"], 20: ["max1"], 21: ["norm0", "norm1", "take2"], 22: ["take3"], 25: ["take4", "bias0"],
          26: ["bias1"], 27: ["mixa"], 29: ["mixb", "st2"], 31: ["mv2"], 32: ["n2a"], 33: ["take5"],
          34: ["n2b", "hi"], 37: ["lo", "take6"], 38: ["take7"], 42: ["take8"]}
AT_POOL = {0: ["tapsum0"], 5: ["tapsum1"], 7: ["tapsum2"], 14: ["pow1"], 17: ["tail0"], 18: ["tail1"], 24: ["tail2"],
           25: ["add0"], 26: ["add1"], 33: ["add2", "add3"], 37: ["pow2"], 42: ["add4", "add5", "add6", "add7"]}
BANK_OF = dict(hid=6, span0=7, span1=6, span2=7, span3=6, span4=7, tT=6, n1T=7, scores0=6, scores1=7, probT0=7,
               attn0=7, probT1=6, attn1=6, gates0=7, gates1=6, t2T=6, hl=7, logits=7, gT=7)
FIRST_BANK = dict(hid=6, span0=0, span1=1, span2=2, span3=3, span4=5, tT=7, n1T=6, scores0=0, scores1=1, probT0=2,
                  attn0=3, probT1=5, attn1=7, gates0=6, gates1=0, t2T=1, hl=7, lh=6)
GN_BANK = (0, 5)
WARM_BANK = 4
FRONT_PE = ["hid", "span0", "span1", "span2", "span3", "span4", "tT", "n1T", "scores0", "scores1", "probT0",
            "attn0", "probT1", "attn1", "gates0", "gates1", "t2T", "hl", "lh"]
FRONT_ACT = ["hid", "t_tok", "k", "exp0", "exp1", "probT0", "attn0", "probT1", "attn1", "tanh", "res", "hl", "lh"]
FRONT_DVE = ["hid_lo", *(f"tap{k}" for k in range(TAPS)), "st1", "mv1", "n1a", "n1b", "q", "max0", "max1",
             "norm0", "norm1", "bias0", "bias1", "mixa", "mixb", "st2", "mv2", "n2a", "n2b", "hi", "lo"]
FRONT_POOL = ["pow1", "pow2"]
GATE_ORDER = [0, *range(EXPERTS, GATES), *range(1, EXPERTS)]

EMPTIED = dict(hid=("hid_ready", 2, 2), tT=("t_tok_ready", 1, 1), n1T=("q_ready", 1, 1), t2T=("res_ready", 1, 1),
               hl=("hl_sb", 1, 1), lh=("x_first", 2, 2), logits=("shifted", 1, 1), gT=("gT_sb", 1, 1))
EMPTIED.update({f"span{i}": ("taps_ready", TAPS, min(2 * i + 2, TAPS)) for i in range(5)})
for _r in range(2):
    EMPTIED.update({f"scores{_r}": ("exp_ready", 4, 2 * _r + 2), f"probT{_r}": ("probT_sb", 2, _r + 1),
                    f"attn{_r}": ("cat_attn", 2, _r + 1), f"gates{_r}": ("zrf_ready", 2, _r + 1)})


def bank_of(name, n):
    return FIRST_BANK[name] if isinstance(n, int) and name in FIRST_BANK else BANK_OF[name]


def piece_at(i):
    return bass.ts(i % 2 * (PIECES // 2) + i // 2, PIECE)


def parts_of(m):
    return min(TAIL_EXPERTS, EXPERTS - m * TAIL_EXPERTS)


def of_block(name):
    return name in ROUTER or name.rstrip("0123456789") in ("take", "add", "tail")


FIRST, OTHERS = slice(0, 1), slice(1, BLOCKS)
PRO_HIGHS = [7, 5, 4, 0, 0, 0, 0, 0, 0, 0, 0, 0, 0]
PRO_SPLITS = [7, 0]
EARLY_SPLITS = 4
BETWEEN_NORMS = 3
BY_DVE = (8, 13)
BY_POOL = [i for i in range(PIECES) if i not in BY_DVE]
WARM = dict(start=0, norm=5, hid=2, span4=0, tT=16, n1T=0, others=5, scores1=7, probT0=3, probT1=3, attn1=0,
            gates1=15, t2T=13, lh=2)
ADD_HALVES = {5: 0, 9: 1, 13: 2}


def build(nc, x, packed, wspan, w1, w3, w2, out):
    with ExitStack() as ctx:
        def sb(name, shape, dt=F32, at=ctx):
            return at.enter_context(nc.sbuf_tensor(name, shape, dt))

        bank = [ctx.enter_context(nc.psum_tensor(f"bank{i}", [P, 512], F32)) for i in range(8)]

        par = sb("par", [P, PACKED])
        w13 = sb("w13", [P, 2 * CHUNKS * P], F32R)
        w2_sb = sb("w2_sb", [P, CHUNKS, C])
        span_sb = sb("span_sb", [P, TAPS * P], F32R)
        cols = {name: par[:, at] for name, at in AT_COL.items()}
        ident = cols["ident"]
        xin = sb("xin", [P, BLOCKS, PX])
        xpad = sb("xpad", [P, BLOCKS, PADW, PADW])
        x_hl = sb("x_hl", [P, BLOCKS * TOK], F32R)
        x_lh = sb("x_lh", [P, BLOCKS * TOK], F32R)
        total = sb("total", [P, (BLOCKS - 1) * TOK])
        gn_st = sb("gn_st", [P, BLOCKS, 6])
        gn_mv = sb("gn_mv", [P, BLOCKS, 2])
        gn_avg = sb("gn_avg", [P, BLOCKS, 2])
        gn_d = sb("gn_d", [P, BLOCKS])
        gn_d2 = sb("gn_d2", [P, BLOCKS])
        gn_var = sb("gn_var", [P, BLOCKS])
        gn_rstd = sb("gn_rstd", [P, BLOCKS])
        gn_bias = sb("gn_bias", [P, BLOCKS])
        minus_half = sb("minus_half", [P, TILES])
        hid_raw = sb("hid_raw", [P, PX])
        hid = sb("hid", [P, PX], F32R)
        prod = sb("prod", [P, TAPS, PX])
        tapsum = sb("tapsum", [P, 2, PX])
        conv = sb("conv", [P, 3, PX])
        t_tok = sb("t_tok", [P, TILES, C])
        ln_st = sb("ln_st", [P, 2, TILES, 6])
        ln_mv = sb("ln_mv", [P, 2, TILES, 2])
        ln_ve = sb("ln_ve", [P, 2, TILES])
        ln_rs = sb("ln_rs", [P, 2, TILES])
        spare = sb("spare", [P, 1])
        spare_act = sb("spare_act", [P, 1])
        n1 = sb("n1", [P, TILES, 2, C])
        qT = sb("qT", [P, TOK])
        kT = sb("kT", [P, TOK])
        cat = sb("cat", [P, TOK])
        mx = sb("mx", [P, 2, 2])
        nmx = sb("nmx", [P, 2, 2])
        ssum = sb("ssum", [P, 2, 2])
        rsum = sb("rsum", [P, 2, 2])
        prob = sb("prob", [P, 2, 2, PX])
        probT = sb("probT", [P, 2, 2, PX])
        zrf = sb("zrf", [P, TILES, 3 * C])
        gu = sb("gu", [P, TILES, C])
        gv = sb("gv", [P, TILES, C])
        t2 = sb("t2", [P, TILES, 2 * C])
        res = sb("res", [P, TOK])
        n2 = sb("n2", [P, TILES, C])
        hlh = sb("hlh", [P, TILES, 3 * C])
        hl_next = sb("hl_next", [P, TOK], F32R)
        rt = sb("rt", [P, 4, TILES, EXPERTS])
        rs = sb("rs", [P, 5, TILES])
        rprob = sb("rprob", [P, TILES, 2 * EXPERTS])
        rmax = sb("rmax", [P, TILES, 8])
        rtop = sb("rtop", [P, TILES, 8])
        rrest = sb("rrest", [P, TILES, 2 * EXPERTS])
        logitsT = sb("logitsT", [P, TOK])
        gT = sb("gT", [TILES * EXPERTS, P])
        gates_dram = nc.dram_tensor("gates_dram", (EXPERTS, TILES, P), F32).ap()
        raw = ExitStack()
        stage = sb("stage", [P, PIECES, PIECE], at=raw)
        span_raw = sb("span_raw", [P, TAPS * P], at=raw)
        raw.close()
        def hidden(s):
            e, m = SEQ[s]
            return htail[:, m, :] if e is None else hbuf[:, (s - TAILS) % SLOTS, :]
        hbuf = sb("hbuf", [P, SLOTS, TOK])
        htail = sb("htail", [P, TAILS, TOK])
        gbc = sb("gbc", [P, GATES, TOK])
        ysc = sb("ysc", [P, 2, TOK])
        ysum = sb("ysum", [P, TOK])
        y_out = sb("y_out", [C, BLOCKS, TOK])

        names = """early_in span_in late_in w2_in x_hl_in x_lh_in
        pads_zero consts_set gn_stats gn_means gn_avg_ready gn_avg_sb gn_d_ready gn_d2_ready
        gn_var_ready gn_rstd_ready gn_bias_ready xn_ready span_high span_split w_high w_split w_split_dve
        hidp_ready hid_ready hid_split kmap_ready taps_ready tapsum_ready conv_ready tT_ready t_tok_ready
        st_ready mv_ready ve_ready rstd_ready n1_ready n1T_ready q_ready k_ready scores_ready mx_ready nmx_ready
        exp_ready rsum_ready prob_ready probT_ready probT_sb attn_ready cat_attn gates_ready zrf_ready tanh_ready
        gu_ready gv_ready gw_ready t2_ready t2T_ready res_ready n2_ready hi_ready hi_again lo_ready hl_ready lh_ready hl_sb
        logits_sb logits_ready shifted rexp_ready routed rgates_ready gT_ready gT_sb
        up_ready silu_ready h_ready tail_gated down_done gates_stored gates_zero out_taken out_added block_summed
        fold_ready y_ready stored x_first upper_in last_ready""".split()
        S = {n: ctx.enter_context(nc.semaphore(n)) for n in names}
        x_in = [ctx.enter_context(nc.semaphore(f"x_in{p}")) for p in range(BLOCKS)]
        stage_in = [ctx.enter_context(nc.semaphore(f"stage_in{i}")) for i in range(PIECES)]
        gate_in = [ctx.enter_context(nc.semaphore(f"gate_in{i}")) for i in range(GATES)]
        block = ctx.enter_context(nc.Block())

        def run_stages(stages, at, step, tb, front):
            for name in at.get(step, ()):
                if of_block(name):
                    stages(name, tb)
                elif front:
                    stages(name, tb + 1)

        @block.sync
        def _(sp):
            sp.sem_inc(S["x_hl_in"], CREDIT)
            sp.sem_inc(S["x_lh_in"], CREDIT)
            sp.sem_inc(S["gates_stored"], CREDIT)

            def load_x(p):
                sp.dma_start(xin[:, p, :], x[2 * p:2 * p + 2].rearrange("b c s -> (b c) s")).then_inc(x_in[p], 16)
            load_x(0)
            sp.dma_start(par[:, 0:EARLY], packed[:, 0:EARLY]).then_inc(S["early_in"], 16)
            sp.dma_start(span_raw[:], wspan).then_inc(S["span_in"], 16)
            for p in range(1, BLOCKS):
                load_x(p)
            sp.dma_start(par[:, EARLY:PACKED], packed[:, EARLY:PACKED]).then_inc(S["late_in"], 16)
            for i in range(PIECES):
                src = (w1, w3)[i % 2][:, bass.ts(i // 2, PIECE)]
                sp.dma_start(stage[:, i, :], src).then_inc(stage_in[i], 16)
                if i == PIECES - 1:
                    sp.dma_start(w2_sb[:], w2.rearrange("p (k c) -> p k c", c=C)).then_inc(S["w2_in"], 16)

            sp.wait_ge(S["gates_zero"], TAILS)

            def spread_gates(n):
                sp.wait_ge(S["gT_sb"], n + 1)
                sp.wait_ge(S["out_taken"], CREDIT + n * OUTS)
                sp.wait_ge(S["tail_gated"], CREDIT + n * TAILS)
                sp.dma_start(gates_dram.rearrange("e t p -> t e p"),
                             gT[:]).then_inc(S["gates_stored"], 16)
                sp.wait_ge(S["gates_stored"], CREDIT + 16 * (n + 1))
                for i in GATE_ORDER:
                    if i < EXPERTS:
                        sp.dma_start(gbc[:, i, :], gates_dram[i].rearrange("t p -> (t p)").partition_broadcast(P)).then_inc(gate_in[i], 16)
                    else:
                        first = (i - EXPERTS) * TAIL_EXPERTS
                        for e in range(first, min(first + TAIL_EXPERTS, EXPERTS)):
                            sp.dma_start(gbc[rest_row(e):rest_row(e) + REST, i, :],
                                         gates_dram[e].rearrange("t p -> (t p)").partition_broadcast(REST)).then_inc(gate_in[i], 16)

            def place_tokens(n):
                there = bass.ds(sp.snap(n * TOK), TOK)
                sp.wait_ge(S["hl_sb"], n + 1)
                sp.dma_start(x_hl[:, there].bitcast(F32), hl_next[:].bitcast(F32)).then_inc(S["x_hl_in"], 16)
                for h in range(2):
                    sp.dma_start(x_lh[h * C:(h + 1) * C, there].bitcast(F32),
                                 hl_next[(1 - h) * C:(2 - h) * C, :].bitcast(F32)).then_inc(S["x_lh_in"], 16)

            with sp.Fori(0, BLOCKS - 1) as tb:
                spread_gates(tb)
                place_tokens(tb + 1)
            sp.wait_ge(S["block_summed"], CREDIT + BLOCKS - 1)
            sp.dma_start(y_out[:, 0:BLOCKS - 1, :], total[C:P, :].rearrange("c (p s) -> c p s", s=TOK)).then_inc(S["upper_in"], 16)
            spread_gates(BLOCKS - 1)
            for p in range(BLOCKS - 1):
                sp.wait_ge(S["y_ready"], p + 1)
                sp.dma_start(out[2 * p:2 * p + 2].rearrange("b c s -> c b s"),
                             y_out[:, p, :].rearrange("c (b s) -> c b s", b=2)).then_inc(S["stored"], 16)
            for h in range(2):
                sp.wait_ge(S["last_ready"], h + 1)
                sp.dma_start(out[2 * (BLOCKS - 1) + h], y_out[:, BLOCKS - 1, h * PX:(h + 1) * PX]).then_inc(S["stored"], 16)
            sp.wait_ge(S["stored"], 16 * (BLOCKS + 1))

        @block.gpsimd
        def _(pool):
            g = nc.gpsimd
            pool.sem_inc(S["tail_gated"], CREDIT)
            pool.sem_inc(S["out_added"], CREDIT)
            pool.sem_inc(S["tapsum_ready"], 3)
            g.memset(minus_half[:], -0.5).then_inc(S["consts_set"], 1)
            g.memset(xpad[:].rearrange("p a y x -> p (a y x)"), 0.0).then_inc(S["pads_zero"], 1)
            g.memset(t2[:, :, C:2 * C], 0.0).then_inc(S["consts_set"], 1)
            g.memset(rprob[:, :, EXPERTS:2 * EXPERTS], -1.0).then_inc(S["consts_set"], 1)
            g.memset(rtop[:, :, 2:8], -1.0).then_inc(S["consts_set"], 1)
            pool.wait_ge(S["consts_set"], 4)
            g.memset(kT[C:P, :], 1.0).then_inc(S["consts_set"], 1)
            pool.wait_ge(S["consts_set"], 5)

            def group_norm(blocks, part):
                pool.wait_ge(S["gn_var_ready"], part)
                g.tensor_tensor(gn_rstd[:, blocks], gn_var[:, blocks], minus_half[:, blocks],
                                ALU.pow).then_inc(S["gn_rstd_ready"], 1)
                pool.wait_ge(S["gn_rstd_ready"], part)
            group_norm(FIRST, 1)

            def stages(name, n):
                if name[:4] == "tail":
                    m = int(name[4:])
                    pool.wait_ge(S["h_ready"], CREDIT + n * CHUNKS + POS[(None, m)] + 1)
                    pool.wait_ge(gate_in[EXPERTS + m], 16 * parts_of(m) * (n + 1))
                    g.tensor_tensor(htail[:, m, :], htail[:, m, :], gbc[:, EXPERTS + m, :],
                                    ALU.mult).then_inc(S["tail_gated"], 1)
                elif name[:3] == "add":
                    i = int(name[3:])
                    pool.wait_ge(S["out_taken"], CREDIT + n * OUTS + i + 1)
                    if i:
                        pool.wait_ge(S["out_added"], CREDIT + n * (OUTS - 1) + i)
                    else:
                        pool.wait_ge(S["block_summed"], CREDIT + n)
                        pool.wait_ge(S["res_ready"], n + 1)
                    g.tensor_tensor(ysum[:], ysum[:] if i else res[:], ysc[:, i % 2, :],
                                    ALU.add).then_inc(S["out_added"], 1)
                elif name[:6] == "tapsum":
                    i = int(name[6:])
                    pool.wait_ge(S["taps_ready"], n * TAPS + 2 * (i + 2))
                    if i:
                        pool.wait_ge(S["tapsum_ready"], n * 3 + i)
                        first = tapsum[:]
                    else:
                        first = prod[:, 0:2, :]
                    g.tensor_tensor(tapsum[:], first, prod[:, 2 * i + 2:2 * i + 4, :], ALU.add).then_inc(S["tapsum_ready"], 1)
                else:
                    i = int(name[3:]) - 1
                    pool.wait_ge(S["ve_ready"], 2 * n + i + 1)
                    g.tensor_tensor(ln_rs[:, i], ln_ve[:, i], minus_half[:], ALU.pow).then_inc(S["rstd_ready"], 1)

            done = 0

            def split(count):
                nonlocal done
                for i in BY_POOL[done:done + count]:
                    pool.wait_ge(S["w_high"], i + 1)
                    at = piece_at(i)
                    g.tensor_tensor(w13[C:P, at], stage[C:P, i, :], w13[C:P, at].bitcast(F32),
                                    ALU.subtract).then_inc(S["w_split"], 1)
                done += count
            split(EARLY_SPLITS)
            pool.wait_ge(S["w_split"], done)
            for name, count in zip(FRONT_POOL, PRO_SPLITS):
                stages(name, 0)
                if name == "pow1":
                    pool.wait_ge(S["rstd_ready"], 1)
                    split(BETWEEN_NORMS)
                    pool.wait_ge(S["w_split"], done)
                    group_norm(OTHERS, 2)
                if count:
                    split(count)
                    pool.wait_ge(S["w_split"], done)
            assert done == len(BY_POOL)

            pool.wait_ge(S["w_high"], PIECES)
            pool.wait_ge(S["span_split"], 1)
            pool.wait_ge(S["w_split_dve"], len(BY_DVE))
            for m in range(TAILS):
                g.memset(gbc[:, EXPERTS + m, :], 0.0).then_inc(S["gates_zero"], 1)

            def experts(tb, front):
                for s in range(CHUNKS):
                    run_stages(stages, AT_POOL, s, tb, front)

            with pool.Fori(0, BLOCKS - 1) as tb:
                experts(tb, True)
            experts(BLOCKS - 1, False)

        @block.scalar
        def _(act):
            a = nc.scalar
            act.sem_inc(S["hl_sb"], 1)
            act.sem_inc(S["silu_ready"], CREDIT)
            act.wait_ge(S["span_in"], 16)
            a.copy(span_sb[:], span_raw[:]).then_inc(S["span_high"], 1)

            def stages(name, n):
                if name == "hid":
                    act.wait_ge(S["hidp_ready"], n + 1)
                    a.activation(hid[:], bank[bank_of("hid", n)][:, 0:PX], ACT.Relu, bias=cols["bred"]).then_inc(S["hid_ready"], 1)
                    a.activation(hid_raw[:], bank[bank_of("hid", n)][:, 0:PX], ACT.Relu, bias=cols["bred"]).then_inc(S["hid_ready"], 1)
                elif name == "t_tok":
                    act.wait_ge(S["tT_ready"], n + 1)
                    a.copy(t_tok[:].rearrange("p (b h) c -> p h b c", b=2),
                           bank[bank_of("tT", n)][:, 0:PX].rearrange("p (h b c) -> p h b c", h=2, b=2)).then_inc(S["t_tok_ready"], 1)
                elif name == "k":
                    act.wait_ge(S["n1T_ready"], n + 1)
                    a.copy(kT[0:C, :], bank[bank_of("n1T", n)][0:C, :]).then_inc(S["k_ready"], 1)
                    act.wait_ge(S["k_ready"], 2 * n + 1)
                    a.copy(cat[0:C, :], kT[0:C, :]).then_inc(S["k_ready"], 1)
                elif name[:3] == "exp":
                    r = int(name[3:])
                    act.wait_ge(S["nmx_ready"], 2 * n + r + 1)
                    for i in range(2):
                        a.activation(prob[:, r, i, :], bank[bank_of(f"scores{r}", n)][:, i * PX:(i + 1) * PX], ACT.Exp,
                                     bias=nmx[:, r, i:i + 1], accum_out=ssum[:, r, i:i + 1]).then_inc(S["exp_ready"], 1)
                elif name[:5] == "probT":
                    r = int(name[5:])
                    act.wait_ge(S["probT_ready"], 2 * n + r + 1)
                    a.copy(probT[:, r].rearrange("p j i -> p (j i)"), bank[bank_of(name, n)][:]).then_inc(S["probT_sb"], 1)
                elif name[:4] == "attn":
                    r = int(name[4:])
                    act.wait_ge(S["attn_ready"], 2 * n + r + 1)
                    a.copy(cat[C:P, r * PX:(r + 1) * PX], bank[bank_of(name, n)][C:P, 0:PX]).then_inc(S["cat_attn"], 1)
                elif name == "tanh":
                    act.wait_ge(S["zrf_ready"], 2 * n + 2)
                    a.activation(zrf[:, :, 0:C], zrf[:, :, 0:C], ACT.Tanh).then_inc(S["tanh_ready"], 1)
                    a.activation(zrf[:, :, C:3 * C], zrf[:, :, C:3 * C], ACT.Tanh, scale=0.5).then_inc(S["tanh_ready"], 1)
                elif name == "res":
                    act.wait_ge(S["t2T_ready"], n + 1)
                    a.copy(res[:], bank[bank_of("t2T", n)][:]).then_inc(S["res_ready"], 1)
                elif name in ("hl", "lh"):
                    act.wait_ge(S[f"{name}_ready"], n + 1)
                    source = bank[bank_of(name, n)]
                    if isinstance(n, int):
                        a.copy((x_hl if name == "hl" else x_lh)[:, 0:TOK], source[:]).then_inc(S["x_first"], 1)
                    else:
                        act.wait_ge(S["x_hl_in"], CREDIT + 16 * (n - 1))
                        act.wait_ge(S["x_lh_in"], CREDIT + 32 * (n - 1))
                    if not isinstance(n, int):
                        a.copy(hl_next[:], bank[bank_of("hl", n)][:]).then_inc(S["hl_sb"], 1)
                elif name == "rexp":
                    act.wait_ge(S["shifted"], n + 1)
                    a.activation(rt[:, 1], rt[:, 0], ACT.Exp).then_inc(S["rexp_ready"], 1)
                elif name == "gT":
                    act.wait_ge(S["gT_ready"], n + 1)
                    act.wait_ge(S["gates_stored"], CREDIT + 16 * n)
                    a.copy(gT[:], bank[bank_of("gT", n)][0:TILES * EXPERTS, 0:P]).then_inc(S["gT_sb"], 1)
                else:
                    raise KeyError(name)

            done = 0

            def high(count):
                nonlocal done
                for i in range(done, done + count):
                    act.wait_ge(stage_in[i], 16)
                    at = piece_at(i)
                    a.copy(w13[:, at], stage[:, i, :]).then_inc(S["w_high"], 1)
                done += count
            for name, count in zip(FRONT_ACT, PRO_HIGHS):
                stages(name, 0)
                if name == "tanh":
                    a.activation(spare_act[:], ln_rs[:, 0, 0:1], ACT.Silu)
                high(count)
            assert done == PIECES

            def experts(tb, front):
                for s in range(CHUNKS):
                    act.wait_ge(S["up_ready"], tb * 2 * CHUNKS + 2 * s + 1)
                    act.wait_ge(S["down_done"], CREDIT + tb * CHUNKS + freed_by(s))
                    a.activation(hidden(s), bank[s % 2][:], ACT.Silu).then_inc(S["silu_ready"], 1)
                    if s == 0:
                        act.wait_ge(S["logits_ready"], CREDIT + tb)
                        a.copy(logitsT[:], bank[0][:]).then_inc(S["logits_sb"], 1)
                    run_stages(stages, AT_ACT, s, tb, front)

            with act.Fori(0, BLOCKS - 1) as tb:
                experts(tb, True)
            experts(BLOCKS - 1, False)
            for h in range(2):
                act.wait_ge(S["fold_ready"], h + 1)
                a.copy(y_out[:, BLOCKS - 1, h * PX:(h + 1) * PX], bank[6 + h][0:C, 0:PX]).then_inc(S["last_ready"], 1)

        @block.vector
        def _(dve):
            v = nc.vector
            dve.sem_inc(S["h_ready"], CREDIT)
            dve.sem_inc(S["out_taken"], CREDIT)
            dve.sem_inc(S["conv_ready"], 3)
            dve.sem_inc(S["block_summed"], CREDIT)
            def gn_means(blocks, part):
                for p in range(blocks.start, blocks.stop):
                    dve.wait_ge(x_in[p], 16)
                    v.bn_stats(gn_st[:, p], xin[:, p, :]).then_inc(S["gn_stats"], 1)
                for p in range(blocks.start, blocks.stop):
                    dve.wait_ge(S["gn_stats"], p + 1)
                    v.bn_aggr(gn_mv[:, p], gn_st[:, p]).then_inc(S["gn_means"], 1)

            def gn_variance(blocks, part):
                dve.wait_ge(S["gn_avg_ready"], part)
                count = blocks.stop - blocks.start
                v.tensor_copy(gn_avg[:, blocks].rearrange("p a b -> p (a b)"),
                              bank[GN_BANK[part - 1]][:, 0:2 * count]).then_inc(S["gn_avg_sb"], 1)
                dve.wait_ge(S["gn_avg_sb"], part)
                v.tensor_tensor(gn_d[:, blocks], gn_mv[:, blocks, 0], gn_avg[:, blocks, 0], ALU.subtract).then_inc(S["gn_d_ready"], 1)
                dve.wait_ge(S["gn_d_ready"], part)
                v.tensor_tensor(gn_d2[:, blocks], gn_d[:, blocks], gn_d[:, blocks], ALU.mult).then_inc(S["gn_d2_ready"], 1)
                dve.wait_ge(S["gn_d2_ready"], part)
                v.scalar_tensor_tensor(gn_var[:, blocks], gn_d2[:, blocks], 1e-5, gn_avg[:, blocks, 1],
                                       ALU.add, ALU.add).then_inc(S["gn_var_ready"], 1)

            def gn_apply(blocks, part):
                dve.wait_ge(S["gn_rstd_ready"], part)
                v.scalar_tensor_tensor(gn_bias[:, blocks], gn_avg[:, blocks, 0], -1.0, gn_rstd[:, blocks],
                                       ALU.mult, ALU.mult).then_inc(S["gn_bias_ready"], 1)
                dve.wait_ge(S["gn_bias_ready"], part)
                for p in range(blocks.start, blocks.stop):
                    v.tensor_scalar(xpad[:, p, 1:1 + IMG, 1:1 + IMG], xin[:, p, :].rearrange("p (y x) -> p y x", y=IMG),
                                    gn_rstd[:, p:p + 1], gn_bias[:, p:p + 1], ALU.mult, ALU.add).then_inc(S["xn_ready"], 1)

            gn_means(FIRST, 1)
            gn_variance(FIRST, 1)
            dve.wait_ge(S["pads_zero"], 1)
            gn_apply(FIRST, 1)
            dve.wait_ge(S["span_high"], 1)
            v.tensor_tensor(span_sb[C:P, :], span_raw[C:P, :], span_sb[C:P, :].bitcast(F32), ALU.subtract).then_inc(S["span_split"], 1)
            dve.wait_ge(S["xn_ready"], 1)

            LINKS = 8
            link_at = [0]

            def link(n, ins):
                link_at[0] += 1
                ins.then_inc(S["routed"], 1)
                dve.wait_ge(S["routed"], n * LINKS + link_at[0])

            def wide(i):
                return rs[:, i].rearrange("p (t e) -> p t e", e=1).to_broadcast([P, TILES, EXPERTS])

            def stages(name, n):
                if name[:4] == "take":
                    i = int(name[4:])
                    e = OUT_ORDER[i]
                    dve.wait_ge(S["down_done"], CREDIT + n * CHUNKS + LAST_OF[e] + 1)
                    dve.wait_ge(S["out_added"], CREDIT + n * (OUTS - 1) + max(i - 1, 0))
                    if e == TAIL:
                        v.tensor_copy(ysc[:, i % 2, :], bank[4 + i % 2][:]).then_inc(S["out_taken"], 1)
                    elif isinstance(n, int) and i == OUTS - 1:
                        dve.wait_ge(gate_in[e], 16 * (n + 1))
                        for h in range(2):
                            half = slice(h * PX, (h + 1) * PX)
                            v.tensor_tensor(ysc[:, i % 2, half], bank[4 + i % 2][:, half], gbc[:, e, half],
                                            ALU.mult).then_inc(S["out_taken"], 1)
                    else:
                        dve.wait_ge(gate_in[e], 16 * (n + 1))
                        v.tensor_tensor(ysc[:, i % 2, :], bank[4 + i % 2][:], gbc[:, e, :],
                                        ALU.mult).then_inc(S["out_taken"], 1)
                elif name == "hid_lo":
                    dve.wait_ge(S["hid_ready"], 2 * n + 2)
                    for r in (32, 96):
                        v.tensor_tensor(hid[r:r + 32, :], hid_raw[r:r + 32, :], hid[r:r + 32, :].bitcast(F32),
                                        ALU.subtract).then_inc(S["hid_split"], 1)
                elif name[:3] == "tap":
                    k = int(name[3:])
                    dve.wait_ge(S["kmap_ready"], 5 * n + k // 2 + 1)
                    window = xpad[:, n, k // 3:k // 3 + IMG, k % 3:k % 3 + IMG] if isinstance(n, int) else \
                        xpad[:, bass.ds(n, 1), k // 3:k // 3 + IMG, k % 3:k % 3 + IMG].rearrange("p a y x -> p (a y) x")
                    kmap = bank[bank_of(f"span{k // 2}", n)][:, k % 2 * PX:(k % 2 + 1) * PX]
                    v.scalar_tensor_tensor(prod[:, k, :].rearrange("p (y x) -> p y x", y=IMG),
                                           kmap.rearrange("p (y x) -> p y x", y=IMG),
                                           cols["bspan"][:, k:k + 1], window, ALU.add, ALU.mult).then_inc(S["taps_ready"], 1)
                elif name == "res8":
                    source = xin[:, n, :] if isinstance(n, int) else xin[:, bass.ds(n, 1), :].rearrange("p a s -> p (a s)")
                    dve.wait_ge(S["taps_ready"], (n + 1) * TAPS)
                    v.tensor_tensor(conv[:, 0, :], prod[:, TAPS - 1, :], source, ALU.add).then_inc(S["conv_ready"], 1)
                elif name == "conv":
                    dve.wait_ge(S["tapsum_ready"], 3 * n + 3)
                    v.tensor_tensor(conv[:, 1, :], tapsum[:, 0, :], tapsum[:, 1, :], ALU.add).then_inc(S["conv_ready"], 1)
                    dve.wait_ge(S["conv_ready"], 3 * n + 2)
                    v.tensor_tensor(conv[:, 2, :], conv[:, 0, :], conv[:, 1, :], ALU.add).then_inc(S["conv_ready"], 1)
                elif name[:2] in ("st", "mv"):
                    i = int(name[2:]) - 1
                    src, ready = ((t_tok, "t_tok_ready"), (t2, "t2_ready"))[i]
                    if name[:2] == "st":
                        dve.wait_ge(S[ready], n + 1)
                        for t in range(TILES):
                            v.bn_stats(ln_st[:, i, t], src[:, t, 0:C]).then_inc(S["st_ready"], 1)
                        return
                    dve.wait_ge(S["st_ready"], (2 * n + i + 1) * TILES)
                    v.memset(spare[:], 0.0)
                    for t in range(TILES):
                        v.bn_aggr(ln_mv[:, i, t], ln_st[:, i, t]).then_inc(S["mv_ready"], 1)
                    dve.wait_ge(S["mv_ready"], (2 * n + i + 1) * TILES)
                    v.tensor_scalar_add(ln_ve[:, i], ln_mv[:, i, :, 1], 1e-5).then_inc(S["ve_ready"], 1)
                elif name in ("n1a", "n1b"):
                    half = "ab".index(name[-1]) * 2
                    dve.wait_ge(S["rstd_ready"], 2 * n + 1)
                    for t in (half, half + 1):
                        v.tensor_scalar(n1[:, t], t_tok[:, t:t + 1, :].to_broadcast([P, 2, C]), ln_mv[:, 0, t, 0:1],
                                        ln_rs[:, 0, t:t + 1], ALU.subtract, ALU.mult).then_inc(S["n1_ready"], 1)
                elif name == "q":
                    dve.wait_ge(S["k_ready"], 2 * n + 1)
                    v.tensor_scalar(qT[:], bank[bank_of("n1T", n)][:], cols["atts"], cols["attb"], ALU.mult, ALU.add).then_inc(S["q_ready"], 1)
                elif name[:3] == "max":
                    r = int(name[3:])
                    dve.wait_ge(S["scores_ready"], 2 * n + r + 1)
                    v.tensor_reduce(mx[:, r], bank[bank_of(name.replace("max", "scores"), n)][:].rearrange("p (i j) -> p i j", i=2), AX_X, ALU.max).then_inc(S["mx_ready"], 1)
                    dve.wait_ge(S["mx_ready"], 2 * n + r + 1)
                    v.tensor_scalar_mul(nmx[:, r], mx[:, r], -1.0).then_inc(S["nmx_ready"], 1)
                elif name[:4] == "norm":
                    r = int(name[4:])
                    dve.wait_ge(S["exp_ready"], 4 * n + 2 * r + 2)
                    v.reciprocal(rsum[:, r], ssum[:, r]).then_inc(S["rsum_ready"], 1)
                    dve.wait_ge(S["rsum_ready"], 2 * n + r + 1)
                    for i in range(2):
                        v.tensor_scalar_mul(prob[:, r, i, :], prob[:, r, i, :], rsum[:, r, i:i + 1]).then_inc(S["prob_ready"], 1)
                elif name[:4] == "bias":
                    h = int(name[4:])
                    dve.wait_ge(S["gates_ready"], 2 * n + h + 1)
                    v.tensor_tensor(zrf[:, 2 * h:2 * h + 2, :], bank[bank_of(f"gates{h}", n)][:, 0:6 * C].rearrange("p (t c) -> p t c", t=2),
                                    cols["gateb"].rearrange("p (t c) -> p t c", t=1).to_broadcast([P, 2, 3 * C]),
                                    ALU.add).then_inc(S["zrf_ready"], 1)
                elif name == "mixa":
                    dve.wait_ge(S["tanh_ready"], 2 * n + 2)
                    v.scalar_tensor_tensor(gu[:], zrf[:, :, C:2 * C], 1.0, n1[:, :, 0, :], ALU.add, ALU.mult).then_inc(S["gu_ready"], 1)
                    v.scalar_tensor_tensor(gv[:], zrf[:, :, 2 * C:3 * C], 1.0, zrf[:, :, 0:C], ALU.add, ALU.mult).then_inc(S["gv_ready"], 1)
                elif name == "mixb":
                    dve.wait_ge(S["gu_ready"], n + 1)
                    dve.wait_ge(S["gv_ready"], n + 1)
                    v.tensor_tensor(gu[:], gu[:], gv[:], ALU.add).then_inc(S["gw_ready"], 1)
                    dve.wait_ge(S["gw_ready"], n + 1)
                    v.scalar_tensor_tensor(t2[:, :, 0:C], gu[:], 0.5, t_tok[:], ALU.mult, ALU.add).then_inc(S["t2_ready"], 1)
                elif name in ("n2a", "n2b"):
                    half = "ab".index(name[-1]) * 2
                    dve.wait_ge(S["rstd_ready"], 2 * n + 2)
                    for t in (half, half + 1):
                        v.tensor_scalar(n2[:, t, :], t2[:, t, 0:C], ln_mv[:, 1, t, 0:1],
                                        ln_rs[:, 1, t:t + 1], ALU.subtract, ALU.mult).then_inc(S["n2_ready"], 1)
                elif name == "hi":
                    dve.wait_ge(S["n2_ready"], (n + 1) * TILES)
                    high = hlh[:].bitcast(F32R)
                    v.tensor_copy(high[:, :, 0:C], n2[:]).then_inc(S["hi_ready"], 1)
                elif name == "lo":
                    dve.wait_ge(S["hi_ready"], n + 1)
                    v.tensor_tensor(hlh[:, :, C:2 * C], n2[:], hlh[:, :, 0:C], ALU.subtract).then_inc(S["lo_ready"], 1)
                    if isinstance(n, int):
                        v.tensor_copy(hlh[:].bitcast(F32R)[:, :, 2 * C:3 * C], n2[:]).then_inc(S["hi_again"], 1)
                elif name == "shift":
                    link_at[0] = 0
                    dve.wait_ge(S["logits_ready"], CREDIT + n + 1)
                    logits = bank[bank_of("logits", n)][:].rearrange("p (t e) -> p t e", e=P)[:, :, 0:EXPERTS]
                    link(n, v.tensor_reduce(rs[:, 0], logits, AX_X, ALU.max))
                    v.tensor_tensor(rt[:, 0], logits, wide(0), ALU.subtract).then_inc(S["shifted"], 1)
                elif name == "router_a":
                    dve.wait_ge(S["rexp_ready"], n + 1)
                    link(n, v.tensor_reduce(rs[:, 1], rt[:, 1], AX_X, ALU.add))
                    link(n, v.reciprocal(rs[:, 2], rs[:, 1]))
                    link(n, v.tensor_tensor(rprob[:, :, 0:EXPERTS], rt[:, 1], wide(2), ALU.mult))
                elif name == "router_b":
                    v.memset(spare[:], 0.0)
                    for t in range(TILES):
                        last = v.max(rmax[:, t, :], rprob[:, t, 0:EXPERTS])
                    link(n, last)
                    v.tensor_copy(rtop[:, :, 0:2], rmax[:, :, 0:2])
                    link(n, v.scalar_tensor_tensor(rs[:, 3], rmax[:, :, 0], 1e-9, rmax[:, :, 1], ALU.add, ALU.add))
                elif name == "router_c":
                    v.memset(spare[:], 0.0)
                    for t in range(TILES):
                        v.match_replace(rrest[:, t, :], rtop[:, t, :], rprob[:, t, :], 0.0)
                    link(n, v.reciprocal(rs[:, 4], rs[:, 3]))
                elif name == "router_d":
                    link(n, v.tensor_tensor(rt[:, 2], rprob[:, :, 0:EXPERTS], rrest[:, :, 0:EXPERTS], ALU.subtract))
                    assert link_at[0] == LINKS
                    v.tensor_tensor(rt[:, 3], rt[:, 2], wide(4), ALU.mult).then_inc(S["rgates_ready"], 1)
                else:
                    raise KeyError(name)

            def split(pieces):
                for i in pieces:
                    dve.wait_ge(S["w_high"], i + 1)
                    v.tensor_tensor(w13[C:P, piece_at(i)], stage[C:P, i, :], w13[C:P, piece_at(i)].bitcast(F32),
                                    ALU.subtract).then_inc(S["w_split_dve"], 1)

            for name in FRONT_DVE:
                stages(name, 0)
                if name == "n1b":
                    gn_means(OTHERS, 2)
                elif name == "q":
                    gn_variance(OTHERS, 2)
                    split(BY_DVE[:1])
                elif name == "norm1":
                    gn_apply(OTHERS, 2)
                    split(BY_DVE[1:])
            dve.wait_ge(S["xn_ready"], BLOCKS)
            dve.wait_ge(S["consts_set"], 5)

            def experts(tb, front):
                for s in range(CHUNKS):
                    dve.wait_ge(S["silu_ready"], CREDIT + tb * CHUNKS + s + 1)
                    dve.wait_ge(S["up_ready"], tb * 2 * CHUNKS + 2 * s + 2)
                    v.tensor_tensor(hidden(s), hidden(s), bank[2 + s % 2][:], ALU.mult).then_inc(S["h_ready"], 1)
                    run_stages(stages, AT_DVE, s, tb, front)
                    if not front and s in ADD_HALVES:
                        p = ADD_HALVES[s]
                        dve.wait_ge(S["upper_in"], 16)
                        v.tensor_tensor(y_out[:, p, :], y_out[:, p, :], total[0:C, bass.ts(p, TOK)], ALU.add).then_inc(S["y_ready"], 1)
                if not front:
                    return
                dve.wait_ge(S["out_taken"], CREDIT + (tb + 1) * OUTS)
                dve.wait_ge(S["out_added"], CREDIT + (tb + 1) * (OUTS - 1))
                v.tensor_tensor(total[:, bass.ds(tb * TOK, TOK)], ysum[:], ysc[:, (OUTS - 1) % 2, :], ALU.add).then_inc(S["block_summed"], 1)

            with dve.Fori(0, BLOCKS - 1) as tb:
                experts(tb, True)
            experts(BLOCKS - 1, False)

        @block.tensor
        def _(pe):
            t = nc.tensor
            pe.sem_inc(S["down_done"], CREDIT)
            pe.sem_inc(S["logits_ready"], CREDIT)
            pe.wait_ge(S["early_in"], 16)

            def warm(after):
                ones = ident.bitcast(BF16)
                for _ in range(WARM.get(after, 0)):
                    t.matmul(bank[WARM_BANK][:].rearrange("p (a b) -> p a b", a=2), ones[:, 0:P],
                             ones.rearrange("p (a b) -> p a b", a=1).to_broadcast([P, 2, 2 * P]), start=True, stop=True)

            def group_norm(blocks, part):
                pe.wait_ge(S["gn_means"], blocks.stop)
                t.matmul(bank[GN_BANK[part - 1]][:, 0:2 * (blocks.stop - blocks.start)], cols["pairavg"],
                         gn_mv[:, blocks].rearrange("p a b -> p (a b)"), start=True, stop=True).then_inc(S["gn_avg_ready"], 1)
            warm("start")
            group_norm(FIRST, 1)
            warm("norm")

            def emptied(name, n):
                sem, per, at = EMPTIED[name]
                pe.wait_ge(S[sem], n * per + at)

            def stages(name, n):
                into = bank[bank_of(name, n)]
                if name == "hid":
                    pe.wait_ge(S["xn_ready"], 1 if isinstance(n, int) else BLOCKS)
                    window = xpad[:, n, 1:1 + IMG, 1:1 + IMG] if isinstance(n, int) else \
                        xpad[:, bass.ds(n, 1), 1:1 + IMG, 1:1 + IMG]
                    t.matmul(into[:, 0:PX], cols["wred"], window, start=True, stop=True).then_inc(S["hidp_ready"], 1)
                    if isinstance(n, int):
                        for i in range(2):
                            t.matmul(bank[bank_of("tT", n)][:, bass.ts(i, P)], xin[:, n, bass.ts(i, P)], ident,
                                     start=i == 0, stop=False)
                elif name[:4] == "span":
                    i = int(name[4:])
                    if i == 0:
                        pe.wait_ge(S["hid_split"], 2 * n + 2)
                    for k in range(2 * i, min(2 * i + 2, TAPS)):
                        last = t.matmul(into[:, k % 2 * PX:(k % 2 + 1) * PX], span_sb[:, bass.ts(k, P)], hid[:],
                                        start=True, stop=True)
                    last.then_inc(S["kmap_ready"], 1)
                elif name == "tT" and isinstance(n, int):
                    for k in range(TAPS):
                        pe.wait_ge(S["taps_ready"], k + 1)
                        for i in range(2):
                            last = t.matmul(into[:, bass.ts(i, P)], prod[:, k, bass.ts(i, P)], ident,
                                            start=False, stop=k == TAPS - 1 and i == 1)
                    last.then_inc(S["tT_ready"], 1)
                elif name == "tT":
                    pe.wait_ge(S["conv_ready"], 3 * n + 3)
                    for i in range(2):
                        last = t.transpose(into[:, bass.ts(i, P)], conv[:, 2, bass.ts(i, P)], ident)
                    last.then_inc(S["tT_ready"], 1)
                elif name == "n1T":
                    pe.wait_ge(S["n1_ready"], (n + 1) * TILES)
                    for i in range(TILES):
                        last = t.transpose(into[:, bass.ts(i, P)], n1[:, i].rearrange("p a c -> p (a c)"), ident)
                    last.then_inc(S["n1T_ready"], 1)
                elif name[:6] == "scores":
                    r = int(name[6:])
                    pe.wait_ge(S["q_ready"], n + 1)
                    pe.wait_ge(S["k_ready"], 2 * n + 1)
                    for i in range(2):
                        q = r * PX + i * P
                        last = t.matmul(into[:, i * PX:(i + 1) * PX], qT[:, q:q + P], kT[:, r * PX:(r + 1) * PX],
                                        start=True, stop=True)
                    last.then_inc(S["scores_ready"], 1)
                elif name[:5] == "probT":
                    r = int(name[5:])
                    pe.wait_ge(S["prob_ready"], 4 * n + 2 * r + 2)
                    for j in range(2):
                        for i in range(2):
                            o = j * PX + i * P
                            last = t.transpose(into[:, o:o + P], prob[:, r, i, bass.ts(j, P)], ident)
                    last.then_inc(S["probT_ready"], 1)
                elif name[:4] == "attn":
                    r = int(name[4:])
                    pe.wait_ge(S["probT_sb"], 2 * n + r + 1)
                    for j in range(2):
                        last = t.matmul(into[C:P, 0:PX], n1[:, 2 * r + j, 0, :], probT[:, r, j, :],
                                        start=j == 0, stop=j == 1)
                    last.then_inc(S["attn_ready"], 1)
                elif name[:5] == "gates":
                    h = int(name[5:])
                    pe.wait_ge(S["cat_attn"], 2 * n + h + 1)
                    pe.wait_ge(S["k_ready"], 2 * n + 2)
                    for i in range(2):
                        k = (2 * h + i) * P
                        last = t.matmul(into[:, i * 3 * C:(i + 1) * 3 * C], cat[:, k:k + P], cols["gatew"],
                                        start=True, stop=True)
                    last.then_inc(S["gates_ready"], 1)
                elif name == "t2T":
                    pe.wait_ge(S["t2_ready"], n + 1)
                    for i in range(TILES):
                        last = t.transpose(into[:, bass.ts(i, P)], t2[:, i, :], ident)
                    last.then_inc(S["t2T_ready"], 1)
                elif name in ("hl", "lh"):
                    pe.wait_ge(S["lo_ready"], n + 1)
                    if name == "lh":
                        pe.wait_ge(S["hi_again"], n + 1)
                    o = 0 if name == "hl" else C
                    for i in range(TILES):
                        last = t.transpose(into[:, bass.ts(i, P)], hlh[:, i, o:o + P], ident)
                    last.then_inc(S[f"{name}_ready"], 1)
                elif name == "logits":
                    pe.wait_ge(S["logits_sb"], n + 1)
                    for i in range(TILES):
                        last = t.transpose(into[:, bass.ts(i, P)], logitsT[:, bass.ts(i, P)], ident)
                    last.then_inc(S["logits_ready"], 1)
                elif name == "gT":
                    pe.wait_ge(S["rgates_ready"], n + 1)
                    t.transpose(into[0:TILES * EXPERTS, 0:P], rt[:, 3].rearrange("p t e -> p (t e)"),
                                ident).then_inc(S["gT_ready"], 1)
                else:
                    raise KeyError(name)

            before = {}
            for name in FRONT_PE:
                if name == "span0":
                    pe.wait_ge(S["span_split"], 1)
                if name == "n1T":
                    pe.wait_ge(S["late_in"], 16)
                    pe.wait_ge(S["consts_set"], 5)
                if FIRST_BANK[name] in before:
                    emptied(before[FIRST_BANK[name]], 0)
                before[FIRST_BANK[name]] = name
                stages(name, 0)
                warm(name)
                if name == "n1T":
                    group_norm(OTHERS, 2)
                    warm("others")
            pe.wait_ge(S["w2_in"], 16)
            pe.wait_ge(S["w_split"], len(BY_POOL))
            pe.wait_ge(S["w_split_dve"], len(BY_DVE))

            def experts(tb, front):
                here = bass.ds(tb * TOK, TOK)
                before = {}
                for names in AT_PE.values():
                    for name in names:
                        before[BANK_OF[name]] = (name, tb - 1 if of_block(name) else tb)

                def up(s):
                    used = tb * CHUNKS + (s - 1 if s else 0)
                    if s == 2:
                        pe.wait_ge(S["logits_sb"], tb + 1)
                    for w in range(2):
                        pe.wait_ge(S[("silu_ready", "h_ready")[w]], CREDIT + used)
                        col = (w * CHUNKS + column(SEQ[s])) * P
                        dst = bank[2 * w + s % 2]
                        t.matmul(dst[:], w13[:, col:col + P], x_hl[:, here], start=True, stop=False)
                        t.matmul(dst[:], w13[:, col:col + P], x_lh[:, here], start=False, stop=True).then_inc(S["up_ready"], 1)

                def down(d):
                    e, m = DOWNS[d]
                    s = POS[(e, m)]
                    i = OUT_ORDER.index(TAIL if e is None else e)
                    if e is None:
                        pe.wait_ge(S["tail_gated"], CREDIT + tb * TAILS + m + 1)
                    else:
                        pe.wait_ge(S["h_ready"], CREDIT + tb * CHUNKS + s + 1)
                    if m < 2:
                        pe.wait_ge(S["out_taken"], CREDIT + tb * OUTS + max(i - 1, 0))
                    half = d % 2
                    ends = (TAILS if e is None else MAIN) - 2
                    t.matmul(bank[4 + i % 2][half * C:(half + 1) * C, :], w2_sb[:, column(SEQ[s]), :], hidden(s),
                             start=m < 2, stop=m >= ends).then_inc(S["down_done"], 1)

                pe.wait_ge(S["x_first"], 2)
                pe.wait_ge(S["x_hl_in"], CREDIT + 16 * tb)
                pe.wait_ge(S["x_lh_in"], CREDIT + 32 * tb)
                for j in range(0, CHUNKS + 2, 2):
                    for s in (j, j + 1):
                        if s >= CHUNKS:
                            continue
                        up(s)
                        for name in AT_PE.get(s, ()):
                            own = of_block(name)
                            if own or front:
                                n = tb if own else tb + 1
                                emptied(*before[BANK_OF[name]])
                                before[BANK_OF[name]] = (name, n)
                                stages(name, n)
                    for d in downs_at(j):
                        down(d)

            with pe.Fori(0, BLOCKS - 1) as tb:
                experts(tb, True)
            experts(BLOCKS - 1, False)
            for step, (part, sem, count) in enumerate(((ysum[:], "out_added", CREDIT + BLOCKS * (OUTS - 1)),
                                                       (ysc[:, (OUTS - 1) % 2, :], "out_taken", CREDIT + BLOCKS * OUTS))):
                for h in range(2):
                    pe.wait_ge(S[sem], count + step * h)
                    m = t.matmul(bank[6 + h][0:C, 0:PX], cols["fold"], part[:, h * PX:(h + 1) * PX],
                                 start=step == 0, stop=step == 1)
                    if step:
                        m.then_inc(S["fold_ready"], 1)


def _lay_out(i):
    f = np.float32
    x = np.ascontiguousarray(i["x"]).reshape(B, C, PX)
    packed = np.zeros((P, PACKED), f)

    def put(name):
        return packed[:, AT_COL[name]]
    for g in range(P // 2):
        put("pairavg")[2 * g:2 * g + 2, 2 * g:2 * g + 2] = 0.5
    bs = np.asarray(i["L0_conv_b_span"]).reshape(HID, TAPS)
    for r in range(4):
        for b in range(2):
            o = (2 * r + b) * HID
            put("wred")[b * C:(b + 1) * C, o:o + HID] = i["L0_conv_w_reduce"].T
            put("bred")[o:o + HID, 0] = i["L0_conv_b_reduce"]
    for c in range(P):
        put("bspan")[c] = bs[c % C // 4]
    put("ident")[:] = np.eye(P, dtype=f)
    wa, wb, wc = (i["L1_attn_att_w"][k * C:(k + 1) * C] for k in range(3))
    put("atts")[0:C, 0], put("atts")[C:P, 0], put("attb")[0:C, 0] = wc, wa, wb
    for k, n in enumerate("zrf"):
        put("gatew")[:, k * C:(k + 1) * C] = i[f"L1_attn_{n}_w"].T
        put("gateb")[:, k * C:(k + 1) * C] = i[f"L1_attn_{n}_b"][None, :]
    put("fold")[0:C] = put("fold")[C:P] = np.eye(C, dtype=f)
    wspan = np.zeros((P, TAPS, P), f)
    ws = np.asarray(i["L0_conv_w_span"]).reshape(HID, TAPS, HID)
    for r in range(4):
        for b in range(2):
            o = (2 * r + b) * HID
            for c in range(C):
                wspan[o:o + HID, :, b * C + c] = ws[c // 4].T
    def chunks(w, router=None):
        full = np.zeros((CHUNKS * P, C), f)
        full[:EXPERTS * MAIN * P] = w[:, :MAIN * P].reshape(-1, C)
        for e in range(EXPERTS):
            o = column((None, e // TAIL_EXPERTS)) * P + rest_row(e)
            full[o:o + REST] = w[e, MAIN * P:]
        if router is not None:
            o = column((None, ROUTER_CHUNK)) * P
            full[o:o + EXPERTS] = router
        return full
    w1 = chunks(np.asarray(i["L1_ffn_w1"]), np.asarray(i["L1_ffn_router_w"]))
    w3 = chunks(np.asarray(i["L1_ffn_w3"]))
    w1, w3 = (np.tile(w.T, (2, 1)) for w in (w1, w3))
    w2 = chunks(np.asarray(i["L1_ffn_w2"]).transpose(0, 2, 1))
    w2 = np.ascontiguousarray(w2.reshape(CHUNKS, P, C).transpose(1, 0, 2)).reshape(P, CHUNKS * C)
    return {"x": x, "packed": packed, "wspan": wspan.reshape(P, TAPS * P), "w1": w1, "w3": w3,
            "w2": w2}


def kernel(**inputs):
    import concourse.bacc as _bacc
    from concourse.bass_utils import run_bass_kernel_spmd as _run

    arrays = _lay_out({k: np.asarray(a) for k, a in inputs.items()})
    nc = _bacc.Bacc("TRN2", target_bir_lowering=False, num_devices=1)
    args = [nc.dram_tensor(f"in_{k}", a.shape, F32, kind="ExternalInput").ap() for k, a in arrays.items()]
    out = nc.dram_tensor("out", (B, C, PX), F32, kind="ExternalOutput").ap()
    build(nc, *args, out)
    r = _run(nc, [{f"in_{k}": a for k, a in arrays.items()}], core_ids=[0])
    return r.results[0]["out"].reshape(B, C, IMG, IMG)
```
